# Optimizing a Trainium2 kernel written in Bass

```python
import numpy as np
import jax
import jax.numpy as jnp

def _softmax(x, axis=-1):
    return jax.nn.softmax(x, axis=axis)

def _gelu(x):
    return jax.nn.gelu(x, approximate=True)

def _silu(x):
    return jax.nn.silu(x)

def _sigmoid(x):
    return jax.nn.sigmoid(x)

def _layernorm(x, axis=-1, eps=1e-05):
    m = jnp.mean(x, axis=axis, keepdims=True)
    v = jnp.var(x, axis=axis, keepdims=True)
    return (x - m) / jnp.sqrt(v + eps)

def _scatter_add(tgt, idx, src, axis=0):
    return tgt.at[idx].add(src)

def _segment_sum(src, seg, n):
    return jax.ops.segment_sum(src, seg, n)
kernel_name = 'mk_adj_resnorm_d2_adj_r2_c2de1d'

def setup_inputs(seed: int=0):
    np.random.seed(seed)
    _w = jnp.asarray

    def _rec_inputs():
        import jax
        import jax.numpy as jnp
        _gk = jax.random.key(seed)
        x = 7.22e-05 + 1 * jax.random.normal(jax.random.fold_in(_gk, 1), (128, 64, 512), jnp.float32)
        _a = jax.random.bernoulli(jax.random.fold_in(_gk, 2), 0.0625, (64, 64))
        _a = jnp.logical_or(_a, jnp.swapaxes(_a, -1, -2))
        _a = jnp.logical_or(_a, jnp.eye(64, dtype=bool))
        _af = _a.astype(jnp.float32)
        adj = _af
        return (x, adj)
    x, adj = _rec_inputs()

    def _L0_gnn_setup():
        import jax, jax.numpy as jnp
        import numpy as np
        EPS = 1e-08

        def _row_stochastic_causal(A, causal_mask):
            A = A * causal_mask
            deg = jnp.maximum(A.sum(axis=-1, keepdims=True), EPS)
            return A / deg
        key = jax.random.key(seed)
        k = jax.random.split(key, 5)
        B, N, D = (4, 1024, 512)
        s = 1.0 / np.sqrt(D)
        h = jax.random.normal(k[0], (B, N, D), dtype=jnp.float32)
        W_lang = jax.random.normal(k[1], (D, D), dtype=jnp.float32) * s
        W_grav = jax.random.normal(k[2], (D, D), dtype=jnp.float32) * s
        W_V = jax.random.normal(k[3], (D, D), dtype=jnp.float32) * s
        W_O = jax.random.normal(k[4], (D, D), dtype=jnp.float32) * s
        causal_mask = jnp.tril(jnp.ones((N, N), dtype=jnp.float32))
        gate_logit = jnp.zeros((), jnp.float32)
        log_sigma = jnp.zeros((), jnp.float32)
        return {'h': h, 'causal_mask': causal_mask, 'W_lang': W_lang, 'W_grav': W_grav, 'W_V': W_V, 'W_O': W_O, 'gate_logit': gate_logit, 'log_sigma': log_sigma}
    _L0_gnn_all = _L0_gnn_setup()
    _L0_gnn_in = {k: v for k, v in _L0_gnn_all.items() if k in ('W_lang', 'W_grav', 'W_V', 'W_O', 'gate_logit', 'log_sigma')}
    del _L0_gnn_all

    def _L1_gnn_setup():
        import jax, jax.numpy as jnp
        import numpy as np
        DIM = 199
        K_HOP = 3

        def _khop_support(n, k):
            A = np.eye(n, dtype=np.float64)
            idx = np.arange(n)
            A[idx, (idx + 1) % n] = 1.0
            A[(idx + 1) % n, idx] = 1.0
            S = np.linalg.matrix_power(A, k)
            return (S > 0).astype(np.float32)
        key = jax.random.key(seed)
        kx, kk = jax.random.split(key)
        batch, n, f = (128, DIM, 512)
        x = jax.random.normal(kx, (batch, n, f), dtype=jnp.float32)
        support = jnp.asarray(_khop_support(n, K_HOP))
        limit = float(np.sqrt(6.0 / (n + n)))
        kernel = jax.random.uniform(kk, (n, n), minval=-limit, maxval=limit, dtype=jnp.float32)
        bias = jnp.zeros((f,), dtype=jnp.float32)
        return {'x': x, 'support': support, 'kernel': kernel, 'bias': bias}
    _L1_gnn_all = _L1_gnn_setup()
    _L1_gnn_in = {k: v for k, v in _L1_gnn_all.items() if k in ('bias',)}
    del _L1_gnn_all
    return {'x': x, 'adj': adj, 'L0_gnn_W_lang': _L0_gnn_in['W_lang'], 'L0_gnn_W_grav': _L0_gnn_in['W_grav'], 'L0_gnn_W_V': _L0_gnn_in['W_V'], 'L0_gnn_W_O': _L0_gnn_in['W_O'], 'L0_gnn_gate_logit': _L0_gnn_in['gate_logit'], 'L0_gnn_log_sigma': _L0_gnn_in['log_sigma'], 'L1_gnn_bias': _L1_gnn_in['bias']}

def reference(x, adj, L0_gnn_W_lang, L0_gnn_W_grav, L0_gnn_W_V, L0_gnn_W_O, L0_gnn_gate_logit, L0_gnn_log_sigma, L1_gnn_bias):
    import jax
    import jax.numpy as jnp

    def _L0_gnn_ref(h, causal_mask, W_lang, W_grav, W_V, W_O, gate_logit, log_sigma):
        import jax, jax.numpy as jnp
        import numpy as np
        EPS = 1e-08

        def _row_stochastic_causal(A, causal_mask):
            A = A * causal_mask
            deg = jnp.maximum(A.sum(axis=-1, keepdims=True), EPS)
            return A / deg
        z_l = jnp.einsum('bnd,ed->bne', h, W_lang)
        z_g = jnp.einsum('bnd,ed->bne', h, W_grav)
        v = jnp.einsum('bnd,ed->bne', h, W_V)
        N = h.shape[-2]
        not_eye = 1.0 - jnp.eye(N, dtype=h.dtype)
        zn = z_l / jnp.maximum(jnp.linalg.norm(z_l, axis=-1, keepdims=True), EPS)
        A_l = jnp.maximum(jnp.einsum('bnd,bmd->bnm', zn, zn), 0.0) * not_eye
        sq = jnp.sum(z_g * z_g, axis=-1, keepdims=True)
        d2 = jnp.maximum(sq + jnp.swapaxes(sq, -1, -2) - 2.0 * jnp.einsum('bnd,bmd->bnm', z_g, z_g), 0.0)
        sigma = jnp.exp(log_sigma)
        A_g = jnp.exp(-d2 / (2.0 * sigma * sigma)) * not_eye
        K_l = _row_stochastic_causal(A_l, causal_mask)
        K_g = _row_stochastic_causal(A_g, causal_mask)
        w_l = jax.nn.sigmoid(gate_logit)
        K = w_l * K_l + (1.0 - w_l) * K_g
        out = jnp.einsum('bnm,bmd->bnd', K, v)
        return jnp.einsum('bnd,ed->bne', out, W_O)

    def _L1_gnn_ref(x, support, kernel, bias):
        import jax, jax.numpy as jnp
        import numpy as np
        DIM = 199
        K_HOP = 3

        def _khop_support(n, k):
            A = np.eye(n, dtype=np.float64)
            idx = np.arange(n)
            A[idx, (idx + 1) % n] = 1.0
            A[(idx + 1) % n, idx] = 1.0
            S = np.linalg.matrix_power(A, k)
            return (S > 0).astype(np.float32)
        W = support * kernel
        out = jnp.einsum('bnf,nm->bmf', x, W)
        out = out + bias
        return out
    x = _layernorm(x + _L0_gnn_ref(x, adj, L0_gnn_W_lang, L0_gnn_W_grav, L0_gnn_W_V, L0_gnn_W_O, L0_gnn_gate_logit, L0_gnn_log_sigma), axis=-1)
    x = _layernorm(x + _L1_gnn_ref(x, adj, adj, L1_gnn_bias), axis=-1)
    return x

_drawn_inputs = setup_inputs


def setup_inputs(seed=0):
    import zlib

    import numpy as np

    out = dict(_drawn_inputs(seed))
    spreads = {'L1_gnn_bias': (0.0, 0.1)}
    factors = {}
    for name, (base, spread) in spreads.items():
        noise = np.random.default_rng([zlib.crc32(name.encode()), seed]).standard_normal(out[name].shape)
        drawn = base * np.exp(spread * noise) if base else spread * noise
        out[name] = jnp.asarray(drawn.astype(out[name].dtype))
    for name, factor in factors.items():
        out[name] = (out[name] * factor).astype(out[name].dtype)
    return out
```

```python
from contextlib import ExitStack

import concourse.bass as bass
from concourse import mybir

GRAPHS, NODES, DIM = 128, 64, 512
PART = 128
TOKENS = GRAPHS * NODES
BLOCK = 512
NB = TOKENS // BLOCK
TPB = BLOCK // PART
DC = DIM // PART
TRI = DC * (DC + 1) // 2
FILLS = 2 * DC + TPB
RING = 4
EPS = 1e-8
LN_EPS = 1e-5

(SUM_A, SUM_B, DIAG, SQ, SQ_MAX, GRAV_ROWS, DIAG_R, COS_ROWS, DIST, COS, A_LANG, A_GRAV, DEG,
 DEG_MAX, DEG_INV, FACTOR, SCALED, K_A, K_B) = range(1, 20)
ATTN_STEPS = 19


def tri(i, j):
    return (i * DC - i * (i - 1) // 2 + (j - i)) * PART


def build(nc, x, xT, adj, w_lang, w_grav, w_v, w_oT, gate, log_sigma, bias, consts, out):
    fp32, fp32r = mybir.dt.float32, mybir.dt.float32r
    ALU, ACT, AX = mybir.AluOpType, mybir.ActivationFunctionType, mybir.AxisListType

    x_blk = x.rearrange("(s t p) d -> s p t d", t=TPB, p=PART)
    out_blk = out.rearrange("(s t p) d -> s p t d", t=TPB, p=PART)

    with ExitStack() as ctx:
        def sb(name, shape, dt=fp32):
            return ctx.enter_context(nc.sbuf_tensor(name, shape, dt))

        def sem(name):
            return ctx.enter_context(nc.semaphore(name))

        h = sb("h", [PART, TPB, DIM])
        hT = sb("hT", [PART, DC, BLOCK])
        hT_hi = [sb(f"hT_hi{p}", [PART, DC, BLOCK], fp32r) for p in range(2)]
        hT_lo = [sb(f"hT_lo{p}", [PART, DC, BLOCK], fp32r) for p in range(2)]
        UT_hi = sb("UT_hi", [PART, DC, 2, BLOCK], fp32r)
        UT_lo = sb("UT_lo", [PART, DC, 2, BLOCK], fp32r)
        y_hi = [sb(f"y_hi{p}", [PART, TPB, DIM], fp32r) for p in range(2)]
        y_lo = [sb(f"y_lo{p}", [PART, TPB, DIM], fp32r) for p in range(2)]
        U_hi = [sb(f"U_hi{w}", [PART, TRI * PART], fp32r) for w in range(2)]
        U_lo = [sb(f"U_lo{w}", [PART, TRI * PART], fp32r) for w in range(2)]
        MT_hi = sb("MT_hi", [PART, DC, DIM], fp32r)
        MT_lo = sb("MT_lo", [PART, DC, DIM], fp32r)
        PT = sb("PT", [PART, TPB, 2, PART])
        S = sb("S", [PART, 2, TPB, NODES])
        D = sb("D", [PART, 2, TPB, NODES])
        K = sb("K", [PART, TPB, PART])
        KT_hi = sb("KT_hi", [PART, TPB, PART], fp32r)
        KT_lo = sb("KT_lo", [PART, TPB, PART], fp32r)
        r = sb("r", [PART, TPB, DIM])
        h1_hi = sb("h1_hi", [PART, TPB, DIM], fp32r)
        h1_lo = sb("h1_lo", [PART, TPB, DIM], fp32r)
        o = sb("o", [PART, TPB, DIM])
        W1 = sb("W1", [PART, PART])
        W1_hi = sb("W1_hi", [PART, PART], fp32r)
        W1_lo = sb("W1_lo", [PART, PART], fp32r)
        cst = sb("cst", [PART, 2 * PART + NODES])
        ident = cst[:, 0:PART]
        same = cst[:, PART:2 * PART]
        eye = cst[:, 2 * PART:2 * PART + NODES]
        adj2 = sb("adj2", [PART, NODES])
        mask = sb("mask", [PART, NODES])
        bias_b = sb("bias_b", [PART, DIM])
        scal = sb("scal", [PART, 2])
        gain = sb("gain", [PART, 2, TPB])
        wtmp = sb("wtmp", [PART, 4])
        neg_c = sb("neg_c", [PART, 1])
        sq = sb("sq", [PART, 2, TPB])
        rq = sb("rq", [PART, TPB])
        rn = sb("rn", [PART, TPB])
        deg = sb("deg", [PART, 2, TPB])
        minus_half = sb("minus_half", [PART, TPB])
        minus_one = sb("minus_one", [PART, TPB])
        ln_eps = sb("ln_eps", [PART, TPB])
        st = [sb(f"st{n}", [PART, TPB, 6]) for n in range(2)]
        mv = [sb(f"mv{n}", [PART, TPB, 2]) for n in range(2)]
        var_e = [sb(f"var_e{n}", [PART, TPB]) for n in range(2)]
        rstd = [sb(f"rstd{n}", [PART, TPB]) for n in range(2)]
        neg_m = [sb(f"neg_m{n}", [PART, TPB]) for n in range(2)]
        shift = [sb(f"shift{n}", [PART, TPB]) for n in range(2)]

        ring = [ctx.enter_context(nc.psum_tensor(f"ring{b}", [PART, BLOCK], fp32))
                for b in range(RING)]
        lowp = ctx.enter_context(nc.psum_tensor("lowp", [PART, TPB, 2, PART], fp32))
        highp = ctx.enter_context(nc.psum_tensor("highp", [PART, TPB, 2, PART], fp32))
        low2 = lowp[:, :, :, :].rearrange("p (b t) w n -> p b (t w n)", b=2)
        high2 = highp[:, :, :, :].rearrange("p (b t) w n -> p b (t w n)", b=2)
        bcast = high2[:, 0, :].rearrange("p (w t n) -> p w t n", w=2, t=TPB)
        KTp = high2[:, 1, :].rearrange("p (t n) -> p t n", t=TPB)

        w_loaded = [sem(f"w_loaded{n}") for n in range(4)]
        small_loaded = sem("small_loaded")
        hT_loaded = sem("hT_loaded")
        h_loaded = sem("h_loaded")
        out_stored = sem("out_stored")
        w_hi_ready = sem("w_hi_ready")
        w_lo_ready = sem("w_lo_ready")
        act_setup = sem("act_setup")
        dve_setup = sem("dve_setup")
        pool_setup = sem("pool_setup")
        hT_hi_ready = sem("hT_hi_ready")
        hT_lo_ready = sem("hT_lo_ready")
        proj_filled = sem("proj_filled")
        proj_hi = sem("proj_hi")
        proj_lo = sem("proj_lo")
        gram_filled = sem("gram_filled")
        gram_taken = sem("gram_taken")
        pt_filled = sem("pt_filled")
        attn_step = sem("attn_step")
        rnorm_ready = sem("rnorm_ready")
        bcast_filled = sem("bcast_filled")
        exp_ready = sem("exp_ready")
        kt_filled = sem("kt_filled")
        kt_hi_ready = sem("kt_hi_ready")
        kt_lo_ready = sem("kt_lo_ready")
        ky_filled = sem("ky_filled")
        ky_taken = sem("ky_taken")
        stat = [sem(f"stat{n}") for n in range(2)]
        ln_step = [sem(f"ln_step{n}") for n in range(2)]
        h1_ready = sem("h1_ready")
        h1_lo_ready = sem("h1_lo_ready")
        mix_filled = sem("mix_filled")
        mix_taken = sem("mix_taken")
        out_ready = sem("out_ready")

        SMALL_LOADS = 6

        def ge(eng, semaphore, value):
            if not isinstance(value, int) or value > 0:
                eng.wait_ge(semaphore, value)

        def live(s, back):
            return not isinstance(s, int) or 0 <= s - back < NB

        def pipeline(eng, iteration):
            iteration(0, 0)
            iteration(1, 1)
            with eng.Fori(1, NB // 2 - 1) as i:
                iteration(2 * i, 0)
                iteration(2 * i + 1, 1)
            for s in range(NB - 2, NB + 2):
                iteration(s, s % 2)

        block = ctx.enter_context(nc.Block())

        @block.sync
        def _(sp):
            stage = [r, o, h, r]
            for n, w in enumerate([w_lang, w_grav, w_v]):
                sp.dma_start(stage[n][:, :, :], w.rearrange("(c p) d -> p c d", p=PART))\
                    .then_inc(w_loaded[n], 16)
            sp.dma_start(hT[:, :, :], xT[0]).then_inc(hT_loaded, 16)
            sp.dma_start(cst[:, :], consts).then_inc(small_loaded, 16)
            for g in range(2):
                sp.dma_start(adj2[g * NODES:(g + 1) * NODES, :], adj).then_inc(small_loaded, 16)
            sp.dma_start(bias_b[:, :], bias.to_broadcast([PART, DIM])).then_inc(small_loaded, 16)
            sp.dma_start(scal[:, 0:1], gate.to_broadcast([PART, 1])).then_inc(small_loaded, 16)
            sp.dma_start(scal[:, 1:2], log_sigma.to_broadcast([PART, 1])).then_inc(small_loaded, 16)
            sp.wait_ge(w_lo_ready, DC)
            sp.dma_start(r[:, :, :], w_oT.rearrange("(c p) d -> p c d", p=PART))\
                .then_inc(w_loaded[3], 16)
            sp.wait_ge(hT_lo_ready, 1)
            sp.dma_start(hT[:, :, :], xT[1]).then_inc(hT_loaded, 16)

            def iteration(s, p):
                if live(s, -2):
                    sp.wait_ge(hT_lo_ready, s + 2)
                    sp.dma_start(hT[:, :, :], xT[s + 2]).then_inc(hT_loaded, 16)
                if live(s, 2):
                    sp.wait_ge(out_ready, TPB * (s - 1))
                    sp.dma_start(out_blk[s - 2], o[:, :, :]).then_inc(out_stored, 16)
                if live(s, 0):
                    if isinstance(s, int) and s == 0:
                        sp.wait_ge(w_lo_ready, 3 * DC)
                    else:
                        sp.wait_ge(ky_taken, TPB * s)
                    sp.dma_start(h[:, :, :], x_blk[s]).then_inc(h_loaded, 16)

            pipeline(sp, iteration)
            sp.wait_ge(out_stored, 16 * NB)

        @block.tensor
        def _(pe):
            def three_pass(dst, terms, done):
                last = None
                for n, (a_hi, a_lo, b_hi, b_lo) in enumerate(terms):
                    pe.matmul(dst, a_hi, b_hi, start=(n == 0), stop=False)
                    pe.matmul(dst, a_hi, b_lo, start=False, stop=False)
                    last = pe.matmul(dst, a_lo, b_hi, start=False, stop=(n == len(terms) - 1))
                if done is not None:
                    last.then_inc(done, 1)

            fill = 0
            for w in range(2):
                for i in range(DC):
                    ge(pe, proj_lo, fill - RING + 1)
                    terms = []
                    for k in range(DC):
                        sl = slice(i * PART, (i + 1) * PART)
                        terms.append((UT_hi[:, k, w, sl], UT_lo[:, k, w, sl],
                                      UT_hi[:, k, w, i * PART:], UT_lo[:, k, w, i * PART:]))
                    if i == 0:
                        pe.wait_ge(w_lo_ready, DC * (w + 1))
                    three_pass(ring[fill % RING][:, 0:DIM - i * PART], terms, proj_filled)
                    fill += 1
            pe.wait_ge(w_lo_ready, 4 * DC)
            for i in range(DC):
                ge(pe, proj_lo, fill - RING + 1)
                sl = slice(i * PART, (i + 1) * PART)
                three_pass(ring[fill % RING][:, :],
                           [(y_hi[0][:, k, sl], y_lo[0][:, k, sl], y_hi[1][:, k, :], y_lo[1][:, k, :])
                            for k in range(DC)], proj_filled)
                fill += 1

            def project(s, p, w, j):
                n = w * DC + j
                ge(pe, proj_lo, FILLS * (s + 1) + n - RING + 1)
                three_pass(ring[n % RING][:, :],
                           [(U_hi[w][:, tri(i, j):tri(i, j) + PART], U_lo[w][:, tri(i, j):tri(i, j) + PART],
                             hT_hi[p][:, i, :], hT_lo[p][:, i, :]) for i in range(j + 1)], proj_filled)

            def value_tile(s, p, t):
                n = 2 * DC + t
                ge(pe, proj_lo, FILLS * (s + 1) + n - RING + 1)
                sl = slice(t * PART, (t + 1) * PART)
                three_pass(ring[n % RING][:, :],
                           [(hT_hi[p][:, c, sl], hT_lo[p][:, c, sl], MT_hi[:, c, :], MT_lo[:, c, :])
                            for c in range(DC)], proj_filled)

            def iteration(s, p):
                q = 1 - p
                cur, prev, prev2 = live(s, 0), live(s, 1), live(s, 2)
                if cur:
                    pe.wait_ge(hT_lo_ready, s + 1)
                    for j in range(DC - 1):
                        project(s, p, 0, j)
                if prev:
                    pe.wait_ge(gram_taken, s)
                    ge(pe, ky_taken, TPB * (s - 1))
                    for t in range(TPB):
                        for w in range(2):
                            last = pe.transpose(highp[:, t, w, :], PT[:, t, w, :], ident)
                    last.then_inc(pt_filled, 1)
                if cur:
                    project(s, p, 0, DC - 1)
                    for j in range(DC - 1):
                        project(s, p, 1, j)
                if prev:
                    pe.wait_ge(attn_step, ATTN_STEPS * (s - 1) + DIAG_R)
                    pe.matmul(bcast, same, D[:, :, :, :], start=True, stop=True).then_inc(bcast_filled, 1)
                if cur:
                    project(s, p, 1, DC - 1)
                    value_tile(s, p, 0)
                    value_tile(s, p, 1)
                if prev2:
                    if prev:
                        pe.wait_ge(gram_taken, s)
                    for t in range(TPB):
                        pe.wait_ge(h1_lo_ready, TPB * (s - 2) + t + 1)
                        if t >= 2:
                            pe.wait_ge(mix_taken, TPB * (s - 2) + t - 1)
                        three_pass(low2[:, t % 2, :],
                                   [(W1_hi[:, :], W1_lo[:, :], h1_hi[:, t, :], h1_lo[:, t, :])], mix_filled)
                if prev:
                    pe.wait_ge(attn_step, ATTN_STEPS * (s - 1) + K_B)
                    for t in range(TPB):
                        last = pe.transpose(KTp[:, t, :], K[:, t, :], ident)
                    last.then_inc(kt_filled, 1)
                if cur:
                    value_tile(s, p, 2)
                    value_tile(s, p, 3)
                    pe.wait_ge(proj_lo, FILLS * (s + 1) + 2 * DC)
                    ge(pe, mix_taken, TPB * (s - 1))
                    for t in range(TPB):
                        sl = slice(t * PART, (t + 1) * PART)
                        three_pass(lowp[:, t, :, :],
                                   [(hT_hi[p][:, j, sl], hT_lo[p][:, j, sl],
                                     UT_hi[:, j, :, sl], UT_lo[:, j, :, sl]) for j in range(DC)],
                                   gram_filled if t == TPB - 1 else None)
                if prev:
                    pe.wait_ge(kt_lo_ready, s)
                    for t in range(TPB):
                        if t >= 2:
                            pe.wait_ge(ky_taken, TPB * (s - 1) + t - 1)
                        three_pass(high2[:, t % 2, :],
                                   [(KT_hi[:, t, :], KT_lo[:, t, :], y_hi[q][:, t, :], y_lo[q][:, t, :])],
                                   ky_filled)

            pe.wait_ge(small_loaded, 16 * SMALL_LOADS)
            pe.wait_ge(dve_setup, 9)
            pipeline(pe, iteration)

        @block.scalar
        def _(act):
            stage = [r, o, h, r]
            w_hi = [UT_hi[:, :, 0, :], UT_hi[:, :, 1, :], y_hi[0][:, :, :], y_hi[1][:, :, :]]

            def split_weight(n):
                act.wait_ge(w_loaded[n], 16)
                for c in range(DC):
                    act.activation(w_hi[n][:, c, :], stage[n][:, c, :], ACT.Copy).then_inc(w_hi_ready, 1)

            def split_hT(k, p):
                act.wait_ge(hT_loaded, 16 * (k + 1))
                act.activation(hT_hi[p][:, :, :], hT[:, :, :], ACT.Copy).then_inc(hT_hi_ready, 1)

            split_weight(0)
            split_weight(1)
            split_weight(2)
            split_hT(0, 0)
            split_weight(3)
            act.wait_ge(small_loaded, 16 * SMALL_LOADS)
            act.activation(wtmp[:, 0:1], scal[:, 0:1], ACT.Exp, scale=-1.0).then_inc(act_setup, 1)
            act.activation(wtmp[:, 1:2], scal[:, 1:2], ACT.Exp, scale=-2.0).then_inc(act_setup, 1)

            fill = 0
            for w in range(2):
                for i in range(DC):
                    act.wait_ge(proj_filled, fill + 1)
                    act.activation(U_hi[w][:, tri(i, i):tri(i, i) + PART], ring[fill % RING][:, 0:PART],
                                   ACT.Copy, scale=0.5).then_inc(act_setup, 1)
                    if i < DC - 1:
                        act.activation(U_hi[w][:, tri(i, i) + PART:tri(i, i) + (DC - i) * PART],
                                       ring[fill % RING][:, PART:DIM - i * PART], ACT.Copy)\
                            .then_inc(act_setup, 1)
                    fill += 1
            for i in range(DC):
                act.wait_ge(proj_filled, fill + 1)
                act.activation(MT_hi[:, i, :], ring[fill % RING][:, :], ACT.Copy).then_inc(act_setup, 1)
                fill += 1

            def take_hi(s, n, dst):
                act.wait_ge(proj_filled, FILLS * (s + 1) + n + 1)
                act.activation(dst, ring[n % RING][:, :], ACT.Copy).then_inc(proj_hi, 1)

            def norm_tile(k, n, t, dst, src, done):
                act.activation(dst, src, ACT.Identity, bias=shift[n][:, t:t + 1],
                               scale=rstd[n][:, t:t + 1]).then_inc(done, 1)

            def iteration(s, p):
                cur, prev, prev2 = live(s, 0), live(s, 1), live(s, 2)

                def h1_tile(t):
                    if prev2:
                        if t == 0:
                            act.wait_ge(ln_step[0], 4 * (s - 1))
                        norm_tile(s - 2, 0, t, h1_hi[:, t, :], r[:, t, :], h1_ready)
                        norm_tile(s - 2, 0, t, r[:, t, :], r[:, t, :], h1_ready)

                if prev:
                    act.wait_ge(gram_filled, s)
                    act.activation(PT[:, :, :, :], lowp[:, :, :, :], ACT.Copy).then_inc(gram_taken, 1)
                for n in range(2 * DC):
                    if cur:
                        take_hi(s, n, UT_hi[:, n % DC, n // DC, :])
                    if 1 <= n <= TPB:
                        h1_tile(n - 1)
                if prev:
                    act.wait_ge(attn_step, ATTN_STEPS * (s - 1) + DIST)
                    act.activation(S[:, 1, :, :], S[:, 1, :, :], ACT.Exp, scale=neg_c[:, 0:1])\
                        .then_inc(exp_ready, 1)
                if cur:
                    take_hi(s, 2 * DC, y_hi[p][:, 0, :])
                    take_hi(s, 2 * DC + 1, y_hi[p][:, 1, :])
                if live(s, -1):
                    ge(act, gram_filled, s)
                    split_hT(s + 1, 1 - p)
                if prev:
                    act.wait_ge(kt_filled, s)
                    act.activation(KT_hi[:, :, :], KTp, ACT.Copy).then_inc(kt_hi_ready, 1)
                if cur:
                    take_hi(s, 2 * DC + 2, y_hi[p][:, 2, :])
                    take_hi(s, 2 * DC + 3, y_hi[p][:, 3, :])
                if prev2:
                    act.wait_ge(ln_step[1], 4 * (s - 1))
                    for t in range(TPB):
                        norm_tile(s - 2, 1, t, o[:, t, :], o[:, t, :], out_ready)

            act.wait_ge(dve_setup, 9)
            pipeline(act, iteration)

        @block.vector
        def _(dve):
            stage = [r, o, h, r]
            w_hi = [UT_hi[:, :, 0, :], UT_hi[:, :, 1, :], y_hi[0][:, :, :], y_hi[1][:, :, :]]
            w_lo = [UT_lo[:, :, 0, :], UT_lo[:, :, 1, :], y_lo[0][:, :, :], y_lo[1][:, :, :]]

            def split_weight(n):
                for c in range(DC):
                    dve.wait_ge(w_hi_ready, n * DC + c + 1)
                    dve.tensor_tensor(w_lo[n][:, c, :], stage[n][:, c, :], w_hi[n][:, c, :].bitcast(fp32),
                                      ALU.subtract).then_inc(w_lo_ready, 1)

            split_weight(0)
            split_weight(1)
            split_weight(2)
            dve.wait_ge(small_loaded, 16 * SMALL_LOADS)
            dve.wait_ge(pool_setup, 3)
            dve.tensor_tensor(mask[:, :], adj2[:, :], eye, ALU.mult).then_inc(dve_setup, 1)
            dve.wait_ge(dve_setup, 1)
            dve.tensor_tensor(mask[:, :], adj2[:, :], mask[:, :], ALU.subtract).then_inc(dve_setup, 1)
            dve.tensor_tensor(adj2[:, :], adj2[:, :], adj2[:, :], ALU.mult).then_inc(dve_setup, 1)
            dve.wait_ge(dve_setup, 3)
            for g in range(2):
                rows = slice(g * NODES, (g + 1) * NODES)
                dve.tensor_tensor(W1[rows, rows], adj2[rows, :], cst[rows, 2 * PART:2 * PART + NODES],
                                  ALU.add).then_inc(dve_setup, 1)
            dve.wait_ge(dve_setup, 5)
            dve.tensor_copy(W1_hi[:, :], W1[:, :]).then_inc(dve_setup, 1)
            dve.wait_ge(dve_setup, 6)
            dve.tensor_tensor(W1_lo[:, :], W1[:, :], W1_hi[:, :].bitcast(fp32), ALU.subtract)\
                .then_inc(dve_setup, 1)
            split_weight(3)
            dve.wait_ge(act_setup, 2)
            dve.tensor_scalar(neg_c[:, :], wtmp[:, 1:2], -0.5, None, ALU.mult).then_inc(dve_setup, 1)
            dve.tensor_scalar(wtmp[:, 2:3], wtmp[:, 0:1], 1.0, None, ALU.add).then_inc(dve_setup, 1)
            dve.wait_ge(dve_setup, 9)
            dve.reciprocal(wtmp[:, 3:4], wtmp[:, 2:3]).then_inc(dve_setup, 1)
            dve.wait_ge(dve_setup, 10)
            dve.tensor_copy(gain[:, 0, :], wtmp[:, 3:4].to_broadcast([PART, TPB])).then_inc(dve_setup, 1)
            dve.wait_ge(dve_setup, 11)
            dve.tensor_scalar(gain[:, 1, :], gain[:, 0, :], -1.0, 1.0, ALU.mult, ALU.add)\
                .then_inc(dve_setup, 1)

            fill, taken = 0, 2
            for w in range(2):
                for i in range(DC):
                    taken += 1 + (i < DC - 1)
                    dve.wait_ge(act_setup, taken)
                    diag = slice(tri(i, i), tri(i, i) + PART)
                    last = dve.scalar_tensor_tensor(U_lo[w][:, diag], ring[fill % RING][:, 0:PART], 0.5,
                                                    U_hi[w][:, diag].bitcast(fp32), ALU.mult, ALU.subtract)
                    if i < DC - 1:
                        rest = slice(tri(i, i) + PART, tri(i, i) + (DC - i) * PART)
                        last = dve.tensor_tensor(U_lo[w][:, rest], ring[fill % RING][:, PART:DIM - i * PART],
                                                 U_hi[w][:, rest].bitcast(fp32), ALU.subtract)
                    last.then_inc(proj_lo, 1)
                    fill += 1
            for i in range(DC):
                taken += 1
                dve.wait_ge(act_setup, taken)
                dve.tensor_tensor(MT_lo[:, i, :], ring[fill % RING][:, :], MT_hi[:, i, :].bitcast(fp32),
                                  ALU.subtract).then_inc(proj_lo, 1)
                fill += 1

            def take_lo(s, n, dst, hi):
                dve.wait_ge(proj_hi, FILLS * s + n + 1)
                dve.tensor_tensor(dst, ring[n % RING][:, :], hi.bitcast(fp32), ALU.subtract)\
                    .then_inc(proj_lo, 1)

            eye_b = eye.unsqueeze(1).to_broadcast([PART, 2 * TPB, NODES])
            eye_t = eye.unsqueeze(1).to_broadcast([PART, TPB, NODES])
            mask_t = mask[:, :].unsqueeze(1).to_broadcast([PART, TPB, NODES])

            def over_cols(v):
                return v.unsqueeze(2).to_broadcast([PART, v.shape[1], NODES])

            S_all = S[:, :, :, :].rearrange("p w t n -> p (w t) n")
            D_all = D[:, :, :, :].rearrange("p w t n -> p (w t) n")
            sq_all = sq[:, :, :].rearrange("p w t -> p (w t)")
            deg_all = deg[:, :, :].rearrange("p w t -> p (w t)")
            gain_all = gain[:, :, :].rearrange("p w t -> p (w t)")

            def iteration(s, p):
                cur, prev, prev2 = live(s, 0), live(s, 1), live(s, 2)

                def attn(step):
                    dve.wait_ge(attn_step, ATTN_STEPS * (s - 1) + step)

                def take_u(n):
                    if cur:
                        take_lo(s, n, UT_lo[:, n % DC, n // DC, :], UT_hi[:, n % DC, n // DC, :])

                def take_y(t):
                    if cur:
                        take_lo(s, 2 * DC + t, y_lo[p][:, t, :], y_hi[p][:, t, :])

                def statistics(n, k, t, src):
                    dve.bn_stats(st[n][:, t, :], src).then_inc(stat[n], 1)

                def aggregate(n):
                    for t in range(TPB):
                        dve.bn_aggr(mv[n][:, t, :], st[n][:, t, :]).then_inc(stat[n], 1)

                if prev2:
                    dve.wait_ge(stat[0], 2 * TPB * (s - 2) + TPB)
                take_u(0)
                if prev2:
                    aggregate(0)
                take_u(1)
                take_u(2)
                if prev:
                    dve.wait_ge(pt_filled, s)
                    for g in range(2):
                        rows = slice(g * NODES, (g + 1) * NODES)
                        dve.tensor_tensor(S[rows, :, :, :].rearrange("p w t n -> p t w n"),
                                          highp[rows, :, :, rows], PT[rows, :, :, rows], ALU.add)\
                            .then_inc(attn_step, 1)
                    attn(SUM_B)
                    dve.tensor_tensor(D_all, S_all, eye_b, ALU.mult).then_inc(attn_step, 1)
                    attn(DIAG)
                    dve.reduce_sum(sq_all, D_all, AX.X).then_inc(attn_step, 1)
                    attn(SQ)
                    dve.tensor_scalar(rq[:, :], sq[:, 0, :], EPS * EPS, None, ALU.max)\
                        .then_inc(attn_step, 1)
                    dve.scalar_tensor_tensor(S[:, 1, :, :], S[:, 1, :, :], -2.0, over_cols(sq[:, 1, :]),
                                             ALU.mult, ALU.add).then_inc(attn_step, 1)
                take_u(3)
                take_u(4)
                if prev:
                    dve.wait_ge(rnorm_ready, s)
                    dve.tensor_tensor(D[:, 0, :, :], eye_t, over_cols(rn[:, :]), ALU.mult)\
                        .then_inc(attn_step, 1)
                    dve.tensor_tensor(S[:, 0, :, :], S[:, 0, :, :], over_cols(rn[:, :]), ALU.mult)\
                        .then_inc(attn_step, 1)
                take_u(5)
                take_u(6)
                if prev:
                    dve.wait_ge(bcast_filled, s)
                    attn(COS_ROWS)
                    dve.tensor_tensor(S[:, 1, :, :], bcast[:, 1, :, :], S[:, 1, :, :], ALU.add)\
                        .then_inc(attn_step, 1)
                    dve.tensor_tensor(S[:, 0, :, :], bcast[:, 0, :, :], S[:, 0, :, :], ALU.mult)\
                        .then_inc(attn_step, 1)
                    attn(COS)
                    dve.scalar_tensor_tensor(S[:, 0, :, :], S[:, 0, :, :], 0.0, mask_t, ALU.max, ALU.mult)\
                        .then_inc(attn_step, 1)
                take_u(7)
                if prev:
                    dve.wait_ge(exp_ready, s)
                    dve.scalar_tensor_tensor(S[:, 1, :, :], S[:, 1, :, :], 1.0, mask_t, ALU.min, ALU.mult)\
                        .then_inc(attn_step, 1)
                    attn(A_GRAV)
                    dve.reduce_sum(deg_all, S_all, AX.X).then_inc(attn_step, 1)
                    attn(DEG)
                    dve.tensor_scalar(deg_all, deg_all, EPS, None, ALU.max).then_inc(attn_step, 1)
                    attn(DEG_MAX)
                    dve.reciprocal(deg_all, deg_all).then_inc(attn_step, 1)
                    attn(DEG_INV)
                    dve.tensor_tensor(deg_all, deg_all, gain_all, ALU.mult).then_inc(attn_step, 1)
                    attn(FACTOR)
                    dve.tensor_tensor(S_all, S_all, over_cols(deg_all), ALU.mult).then_inc(attn_step, 1)
                    attn(SCALED)
                    for g in range(2):
                        rows = slice(g * NODES, (g + 1) * NODES)
                        dve.tensor_tensor(K[rows, :, rows], S[rows, 0, :, :], S[rows, 1, :, :], ALU.add)\
                            .then_inc(attn_step, 1)
                take_y(0)
                take_y(1)
                if prev2:
                    ge(dve, out_stored, 16 * (s - 2))
                    for t in range(TPB):
                        dve.wait_ge(mix_filled, TPB * (s - 2) + t + 1)
                        dve.tensor_tensor(o[:, t, :], low2[:, t % 2, :], bias_b[:, :], ALU.add)\
                            .then_inc(mix_taken, 1)
                    for t in range(TPB):
                        dve.wait_ge(mix_taken, TPB * (s - 2) + t + 1)
                        statistics(1, s - 2, t, o[:, t, :])
                    dve.wait_ge(stat[1], 2 * TPB * (s - 2) + TPB)
                if prev:
                    dve.wait_ge(kt_hi_ready, s)
                    dve.tensor_tensor(KT_lo[:, :, :], KTp, KT_hi[:, :, :].bitcast(fp32), ALU.subtract)\
                        .then_inc(kt_lo_ready, 1)
                if prev2:
                    aggregate(1)
                take_y(2)
                take_y(3)
                if prev:
                    dve.wait_ge(h_loaded, 16 * s)
                    for t in range(TPB):
                        dve.wait_ge(ky_filled, TPB * (s - 1) + t + 1)
                        dve.tensor_tensor(r[:, t, :], high2[:, t % 2, :], h[:, t, :], ALU.add)\
                            .then_inc(ky_taken, 1)
                    for t in range(TPB):
                        dve.wait_ge(ky_taken, TPB * (s - 1) + t + 1)
                        statistics(0, s - 1, t, r[:, t, :])

            pipeline(dve, iteration)

        @block.gpsimd
        def _(pool):
            pool.memset(W1[:, :], 0.0).then_inc(pool_setup, 1)
            pool.memset(K[:, :, :], 0.0).then_inc(pool_setup, 1)
            pool.memset(minus_half[:, :], -0.5).then_inc(pool_setup, 1)
            pool.memset(minus_one[:, :], -1.0).then_inc(pool_setup, 1)
            pool.memset(ln_eps[:, :], LN_EPS).then_inc(pool_setup, 1)
            pool.wait_ge(pool_setup, 5)

            def split_hT(k, p):
                pool.wait_ge(hT_hi_ready, k + 1)
                pool.tensor_tensor(hT_lo[p][:, :, :], hT[:, :, :], hT_hi[p][:, :, :].bitcast(fp32),
                                   ALU.subtract).then_inc(hT_lo_ready, 1)

            def norm_factors(n, k):
                pool.wait_ge(stat[n], 2 * TPB * (k + 1))
                pool.tensor_tensor(var_e[n][:, :], mv[n][:, :, 1], ln_eps[:, :], ALU.add)\
                    .then_inc(ln_step[n], 1)
                pool.tensor_tensor(neg_m[n][:, :], mv[n][:, :, 0], minus_one[:, :], ALU.mult)\
                    .then_inc(ln_step[n], 1)
                pool.wait_ge(ln_step[n], 4 * k + 2)
                pool.tensor_tensor(rstd[n][:, :], var_e[n][:, :], minus_half[:, :], ALU.pow)\
                    .then_inc(ln_step[n], 1)
                pool.wait_ge(ln_step[n], 4 * k + 3)
                pool.tensor_tensor(shift[n][:, :], neg_m[n][:, :], rstd[n][:, :], ALU.mult)\
                    .then_inc(ln_step[n], 1)

            def iteration(s, p):
                prev, prev2 = live(s, 1), live(s, 2)

                def h1_rest(t):
                    if prev2:
                        pool.wait_ge(h1_ready, 2 * (TPB * (s - 2) + t + 1))
                        pool.tensor_tensor(h1_lo[:, t, :], r[:, t, :], h1_hi[:, t, :].bitcast(fp32),
                                           ALU.subtract).then_inc(h1_lo_ready, 1)

                if prev2:
                    norm_factors(0, s - 2)
                h1_rest(0)
                h1_rest(1)
                if prev:
                    pool.wait_ge(attn_step, ATTN_STEPS * (s - 1) + SQ_MAX)
                    pool.tensor_tensor(rn[:, :], rq[:, :], minus_half[:, :], ALU.pow)\
                        .then_inc(rnorm_ready, 1)
                h1_rest(2)
                h1_rest(3)
                if prev2:
                    norm_factors(1, s - 2)
                if live(s, -1):
                    split_hT(s + 1, 1 - p)

            split_hT(0, 0)
            pipeline(pool, iteration)


def kernel(x, adj, L0_gnn_W_lang, L0_gnn_W_grav, L0_gnn_W_V, L0_gnn_W_O, L0_gnn_gate_logit,
           L0_gnn_log_sigma, L1_gnn_bias):
    import numpy as np
    import concourse.bacc as bacc
    from concourse.bass_utils import run_bass_kernel_spmd

    x = np.ascontiguousarray(x).reshape(TOKENS, DIM)
    same = np.zeros((PART, PART), np.float32)
    for g in range(PART // NODES):
        same[g * NODES:(g + 1) * NODES, g * NODES:(g + 1) * NODES] = 1.0
    arrays = {
        "x": x,
        "xT": np.ascontiguousarray(x.reshape(NB, BLOCK, DC, PART).transpose(0, 3, 2, 1)),
        "adj": np.ascontiguousarray(adj),
        "w_lang": np.ascontiguousarray(L0_gnn_W_lang),
        "w_grav": np.ascontiguousarray(L0_gnn_W_grav),
        "w_v": np.ascontiguousarray(L0_gnn_W_V),
        "w_oT": np.ascontiguousarray(np.asarray(L0_gnn_W_O).T),
        "gate": np.asarray(L0_gnn_gate_logit).reshape(1, 1),
        "log_sigma": np.asarray(L0_gnn_log_sigma).reshape(1, 1),
        "bias": np.ascontiguousarray(L1_gnn_bias).reshape(1, DIM),
        "consts": np.concatenate(
            [np.eye(PART, dtype=np.float32), same,
             np.concatenate([np.eye(NODES, dtype=np.float32)] * (PART // NODES))], axis=1),
    }
    nc = bacc.Bacc("TRN2", target_bir_lowering=False, num_devices=1)
    aps = {n: nc.dram_tensor(n, a.shape, mybir.dt.from_np(a.dtype), kind="ExternalInput").ap()
           for n, a in arrays.items()}
    aps["out"] = nc.dram_tensor("out", (TOKENS, DIM), mybir.dt.float32, kind="ExternalOutput").ap()
    build(nc, **aps)
    res = run_bass_kernel_spmd(nc, [arrays], core_ids=[0])
    return res.results[0]["out"].reshape(GRAPHS, NODES, DIM)
```

```python
from contextlib import ExitStack

import concourse.bass as bass
from concourse import mybir

GRAPHS, NODES, DIM = 128, 64, 512
PART = 128
TOKENS = GRAPHS * NODES
BLOCK = 512
NB = TOKENS // BLOCK
TPB = BLOCK // PART
DC = DIM // PART
TRI = DC * (DC + 1) // 2
FILLS = 2 * DC + TPB
RING = 4
EPS = 1e-8
LN_EPS = 1e-5

(SUM_A, SUM_B, DIAG, SQ, SQ_MAX, GRAV_ROWS, DIAG_R, COS_ROWS, DIAG_LO, DIST, COS, A_LANG, A_GRAV,
 DEG, DEG_MAX, DEG_INV, FACTOR, SCALED, K_A, K_B) = range(1, 21)
ATTN_STEPS = 20


def tri(i, j):
    return (i * DC - i * (i - 1) // 2 + (j - i)) * PART


def build(nc, x, xT, adj, w_lang, w_grav, w_v, w_oT, gate, log_sigma, bias, consts, out):
    fp32, fp32r = mybir.dt.float32, mybir.dt.float32r
    ALU, ACT, AX = mybir.AluOpType, mybir.ActivationFunctionType, mybir.AxisListType

    x_blk = x.rearrange("(s t p) d -> s p t d", t=TPB, p=PART)
    out_blk = out.rearrange("(s t p) d -> s p t d", t=TPB, p=PART)

    with ExitStack() as ctx:
        def sb(name, shape, dt=fp32):
            return ctx.enter_context(nc.sbuf_tensor(name, shape, dt))

        def sem(name):
            return ctx.enter_context(nc.semaphore(name))

        h = sb("h", [PART, TPB, DIM])
        hT = sb("hT", [PART, DC, BLOCK])
        hT_hi = [sb(f"hT_hi{p}", [PART, DC, BLOCK], fp32r) for p in range(2)]
        hT_lo = [sb(f"hT_lo{p}", [PART, DC, BLOCK], fp32r) for p in range(2)]
        UT_hi = sb("UT_hi", [PART, DC, 2, BLOCK], fp32r)
        UT_lo = sb("UT_lo", [PART, DC, 2, BLOCK], fp32r)
        y_hi = sb("y_hi", [PART, TPB, DIM], fp32r)
        y_lo = sb("y_lo", [PART, TPB, DIM], fp32r)
        U_hi = [sb(f"U_hi{w}", [PART, TRI * PART], fp32r) for w in range(2)]
        U_lo = [sb(f"U_lo{w}", [PART, TRI * PART], fp32r) for w in range(2)]
        MT_hi = sb("MT_hi", [PART, DC, DIM], fp32r)
        MT_lo = sb("MT_lo", [PART, DC, DIM], fp32r)
        PT = sb("PT", [PART, TPB, 2, PART])
        S = sb("S", [PART, 2, TPB, NODES])
        D = sb("D", [PART, 2, TPB, NODES])
        D_hi = sb("D_hi", [PART, 2, TPB, NODES], fp32r)
        D_lo = sb("D_lo", [PART, 2, TPB, NODES], fp32r)
        same_r = sb("same_r", [PART, PART], fp32r)
        K = sb("K", [PART, TPB, PART])
        KT_hi = sb("KT_hi", [PART, TPB, PART], fp32r)
        KT_lo = sb("KT_lo", [PART, TPB, PART], fp32r)
        r = sb("r", [PART, TPB, DIM])
        h1_hi = sb("h1_hi", [PART, TPB, DIM], fp32r)
        h1_lo = sb("h1_lo", [PART, TPB, DIM], fp32r)
        o = sb("o", [PART, TPB, DIM])
        w_stage = sb("w_stage", [PART, DC, DIM])
        W1 = sb("W1", [PART, PART])
        W1_hi = sb("W1_hi", [PART, PART], fp32r)
        W1_lo = sb("W1_lo", [PART, PART], fp32r)
        cst = sb("cst", [PART, 2 * PART + NODES])
        ident = cst[:, 0:PART]
        same = cst[:, PART:2 * PART]
        eye = cst[:, 2 * PART:2 * PART + NODES]
        adj2 = sb("adj2", [PART, NODES])
        mask = sb("mask", [PART, NODES])
        bias_b = sb("bias_b", [PART, DIM])
        scal = sb("scal", [PART, 2])
        gain = sb("gain", [PART, 2, TPB])
        wtmp = sb("wtmp", [PART, 4])
        neg_c = sb("neg_c", [PART, 1])
        sq = sb("sq", [PART, 2, TPB])
        rq = sb("rq", [PART, TPB])
        rn = sb("rn", [PART, TPB])
        deg = sb("deg", [PART, 2, TPB])
        anchor = sb("anchor", [PART, 1])
        minus_half = sb("minus_half", [PART, TPB])
        minus_one = sb("minus_one", [PART, TPB])
        ln_eps = sb("ln_eps", [PART, TPB])
        st = [sb(f"st{n}", [PART, TPB, 6]) for n in range(2)]
        mv = [sb(f"mv{n}", [PART, TPB, 2]) for n in range(2)]
        var_e = [sb(f"var_e{n}", [PART, TPB]) for n in range(2)]
        rstd = [sb(f"rstd{n}", [PART, TPB]) for n in range(2)]
        neg_m = [sb(f"neg_m{n}", [PART, TPB]) for n in range(2)]
        shift = [sb(f"shift{n}", [PART, TPB]) for n in range(2)]

        ring = [ctx.enter_context(nc.psum_tensor(f"ring{b}", [PART, BLOCK], fp32))
                for b in range(RING)]
        lowp = ctx.enter_context(nc.psum_tensor("lowp", [PART, TPB, 2, PART], fp32))
        highp = ctx.enter_context(nc.psum_tensor("highp", [PART, TPB, 2, PART], fp32))
        low2 = lowp[:, :, :, :].rearrange("p (b t) w n -> p b (t w n)", b=2)
        high2 = highp[:, :, :, :].rearrange("p (b t) w n -> p b (t w n)", b=2)
        bcast = low2[:, 0, :].rearrange("p (w t n) -> p w t n", w=2, t=TPB)
        mix_bank = [low2[:, 0, :], low2[:, 1, :], high2[:, 0, :], high2[:, 1, :]]
        KTp = high2[:, 1, :].rearrange("p (t n) -> p t n", t=TPB)

        w_loaded = [sem(f"w_loaded{n}") for n in range(4 * DC)]
        small_loaded = sem("small_loaded")
        hT_loaded = sem("hT_loaded")
        h_loaded = sem("h_loaded")
        out_stored = sem("out_stored")
        w_hi_ready = sem("w_hi_ready")
        w_lo_ready = sem("w_lo_ready")
        act_setup = sem("act_setup")
        exps_ready = sem("exps_ready")
        dve_setup = sem("dve_setup")
        pool_setup = sem("pool_setup")
        hT_hi_ready = sem("hT_hi_ready")
        hT_lo_ready = sem("hT_lo_ready")
        proj_filled = sem("proj_filled")
        proj_hi = sem("proj_hi")
        proj_lo = sem("proj_lo")
        gram_filled = sem("gram_filled")
        gram_taken = sem("gram_taken")
        pt_filled = sem("pt_filled")
        attn_step = sem("attn_step")
        diag_hi_ready = sem("diag_hi_ready")
        rnorm_ready = sem("rnorm_ready")
        bcast_filled = sem("bcast_filled")
        exp_ready = sem("exp_ready")
        kt_filled = sem("kt_filled")
        kt_hi_ready = sem("kt_hi_ready")
        kt_lo_ready = sem("kt_lo_ready")
        ky_filled = sem("ky_filled")
        ky_taken = sem("ky_taken")
        stat = [sem(f"stat{n}") for n in range(2)]
        ln_step = [sem(f"ln_step{n}") for n in range(2)]
        h1_ready = sem("h1_ready")
        h1_lo_ready = sem("h1_lo_ready")
        mix_filled = sem("mix_filled")
        mix_taken = sem("mix_taken")
        out_ready = sem("out_ready")

        SMALL_LOADS = 6
        w_raw = [r, o, h, w_stage]
        w_hi = [UT_hi[:, :, 0, :], UT_hi[:, :, 1, :], y_hi[:, :, :], h1_hi[:, :, :]]
        w_lo = [UT_lo[:, :, 0, :], UT_lo[:, :, 1, :], y_lo[:, :, :], h1_lo[:, :, :]]

        def ge(eng, semaphore, value):
            if not isinstance(value, int) or value > 0:
                eng.wait_ge(semaphore, value)

        def live(s, back):
            return not isinstance(s, int) or 0 <= s - back < NB

        def pipeline(eng, iteration):
            iteration(0, 0)
            iteration(1, 1)
            with eng.Fori(1, NB // 2 - 1) as i:
                iteration(2 * i, 0)
                iteration(2 * i + 1, 1)
            for s in range(NB - 2, NB + 2):
                iteration(s, s % 2)

        block = ctx.enter_context(nc.Block())

        @block.sync
        def _(sp):
            def load_weight(n, w):
                for c in range(DC):
                    sp.dma_start(w_raw[n][:, c, :], w[c * PART:(c + 1) * PART, :])\
                        .then_inc(w_loaded[n * DC + c], 16)

            load_weight(0, w_lang)
            load_weight(1, w_grav)
            load_weight(2, w_v)
            load_weight(3, w_oT)
            sp.dma_start(hT[:, :, :], xT[0]).then_inc(hT_loaded, 16)
            sp.dma_start(cst[:, :], consts).then_inc(small_loaded, 16)
            for g in range(2):
                sp.dma_start(adj2[g * NODES:(g + 1) * NODES, :], adj).then_inc(small_loaded, 16)
            sp.dma_start(bias_b[:, :], bias.to_broadcast([PART, DIM])).then_inc(small_loaded, 16)
            sp.dma_start(scal[:, 0:1], gate.to_broadcast([PART, 1])).then_inc(small_loaded, 16)
            sp.dma_start(scal[:, 1:2], log_sigma.to_broadcast([PART, 1])).then_inc(small_loaded, 16)
            sp.wait_ge(hT_lo_ready, 1)
            sp.dma_start(hT[:, :, :], xT[1]).then_inc(hT_loaded, 16)

            def iteration(s, p):
                if live(s, 2):
                    sp.wait_ge(out_ready, TPB * (s - 1))
                    sp.dma_start(out_blk[s - 2], o[:, :, :]).then_inc(out_stored, 16)
                if live(s, -2):
                    sp.wait_ge(hT_lo_ready, s + 2)
                    sp.dma_start(hT[:, :, :], xT[s + 2]).then_inc(hT_loaded, 16)
                if live(s, 0):
                    if isinstance(s, int) and s == 0:
                        sp.wait_ge(w_lo_ready, 3 * DC)
                    else:
                        sp.wait_ge(ky_taken, TPB * s)
                    sp.dma_start(h[:, :, :], x_blk[s]).then_inc(h_loaded, 16)

            pipeline(sp, iteration)
            sp.wait_ge(out_stored, 16 * NB)

        @block.tensor
        def _(pe):
            def three_pass(dst, terms, done, start=True, stop=True):
                last = None
                for n, (a_hi, a_lo, b_hi, b_lo) in enumerate(terms):
                    pe.matmul(dst, a_hi, b_hi, start=(start and n == 0), stop=False)
                    pe.matmul(dst, a_hi, b_lo, start=False, stop=False)
                    last = pe.matmul(dst, a_lo, b_hi, start=False, stop=(stop and n == len(terms) - 1))
                if done is not None:
                    last.then_inc(done, 1)

            fill = 0
            for k in range(DC):
                pe.wait_ge(w_lo_ready, k + 1)
                for i in range(DC):
                    sl = slice(i * PART, (i + 1) * PART)
                    three_pass(ring[i][:, 0:DIM - i * PART],
                               [(UT_hi[:, k, 0, sl], UT_lo[:, k, 0, sl],
                                 UT_hi[:, k, 0, i * PART:], UT_lo[:, k, 0, i * PART:])],
                               proj_filled if k == DC - 1 else None, start=(k == 0), stop=(k == DC - 1))
            fill = DC
            for w in range(1, 2):
                for i in range(DC):
                    ge(pe, proj_lo, fill - RING + 1)
                    terms = []
                    for k in range(DC):
                        sl = slice(i * PART, (i + 1) * PART)
                        terms.append((UT_hi[:, k, w, sl], UT_lo[:, k, w, sl],
                                      UT_hi[:, k, w, i * PART:], UT_lo[:, k, w, i * PART:]))
                    if i == 0:
                        pe.wait_ge(w_lo_ready, DC * (w + 1))
                    three_pass(ring[fill % RING][:, 0:DIM - i * PART], terms, proj_filled)
                    fill += 1
            pe.wait_ge(w_lo_ready, 4 * DC)
            for i in range(DC):
                ge(pe, proj_lo, fill - RING + 1)
                sl = slice(i * PART, (i + 1) * PART)
                three_pass(ring[fill % RING][:, :],
                           [(y_hi[:, k, sl], y_lo[:, k, sl], h1_hi[:, k, :], h1_lo[:, k, :])
                            for k in range(DC)], proj_filled)
                fill += 1

            def project(s, p, w, j):
                n = w * DC + j
                ge(pe, proj_lo, FILLS * (s + 1) + n - RING + 1)
                three_pass(ring[n % RING][:, :],
                           [(U_hi[w][:, tri(i, j):tri(i, j) + PART], U_lo[w][:, tri(i, j):tri(i, j) + PART],
                             hT_hi[p][:, i, :], hT_lo[p][:, i, :]) for i in range(j + 1)], proj_filled)

            def value_tile(s, p, t):
                n = 2 * DC + t
                ge(pe, proj_lo, FILLS * (s + 1) + n - RING + 1)
                sl = slice(t * PART, (t + 1) * PART)
                three_pass(ring[n % RING][:, :],
                           [(hT_hi[p][:, c, sl], hT_lo[p][:, c, sl], MT_hi[:, c, :], MT_lo[:, c, :])
                            for c in range(DC)], proj_filled)

            def gram_tile(s, p, t):
                sl = slice(t * PART, (t + 1) * PART)
                three_pass(lowp[:, t, :, :],
                           [(hT_hi[p][:, j, sl], hT_lo[p][:, j, sl], UT_hi[:, j, :, sl], UT_lo[:, j, :, sl])
                            for j in range(DC)], gram_filled if t == TPB - 1 else None)

            def attend_tile(k, t):
                if t == 0:
                    pe.wait_ge(kt_lo_ready, k + 1)
                if t >= 2:
                    pe.wait_ge(ky_taken, TPB * k + t - 1)
                three_pass(high2[:, t % 2, :],
                           [(KT_hi[:, t, :], KT_lo[:, t, :], y_hi[:, t, :], y_lo[:, t, :])], ky_filled)

            def mix_tile(k, t):
                pe.wait_ge(h1_lo_ready, TPB * k + t + 1)
                three_pass(mix_bank[t],
                           [(W1_hi[:, :], W1_lo[:, :], h1_hi[:, t, :], h1_lo[:, t, :])], mix_filled)

            def iteration(s, p):
                cur, prev = live(s, 0), live(s, 1)
                if cur:
                    pe.wait_ge(hT_lo_ready, s + 1)
                    for j in range(DC):
                        project(s, p, 0, j)
                    project(s, p, 1, 0)
                    project(s, p, 1, 1)
                if prev:
                    pe.wait_ge(attn_step, ATTN_STEPS * (s - 1) + K_B)
                    ge(pe, mix_taken, TPB * (s - 1))
                    for t in range(TPB):
                        last = pe.transpose(KTp[:, t, :], K[:, t, :], ident)
                    last.then_inc(kt_filled, 1)
                if cur:
                    project(s, p, 1, 2)
                    project(s, p, 1, 3)
                if prev:
                    attend_tile(s - 1, 0)
                    attend_tile(s - 1, 1)
                if cur:
                    pe.wait_ge(proj_lo, FILLS * (s + 1) + 2 * DC)
                    gram_tile(s, p, 0)
                if prev:
                    attend_tile(s - 1, 2)
                if cur:
                    gram_tile(s, p, 1)
                if prev:
                    attend_tile(s - 1, 3)
                if cur:
                    gram_tile(s, p, 2)
                    gram_tile(s, p, 3)
                    value_tile(s, p, 0)
                    pe.wait_ge(gram_taken, s + 1)
                    ge(pe, ky_taken, TPB * s)
                    for t in range(TPB):
                        for w in range(2):
                            last = pe.transpose(highp[:, t, w, :], PT[:, t, w, :], ident)
                    last.then_inc(pt_filled, 1)
                    value_tile(s, p, 1)
                if prev:
                    mix_tile(s - 1, 0)
                    mix_tile(s - 1, 1)
                if cur:
                    value_tile(s, p, 2)
                    pe.wait_ge(attn_step, ATTN_STEPS * s + SUM_B)
                if prev:
                    mix_tile(s - 1, 2)
                    mix_tile(s - 1, 3)
                if cur:
                    value_tile(s, p, 3)
                    ge(pe, mix_taken, TPB * (s - 1) + 1)
                    pe.wait_ge(attn_step, ATTN_STEPS * s + DIAG_LO)
                    pe.matmul(bcast, same_r[:, :], D_hi[:, :, :, :], start=True, stop=False)
                    pe.matmul(bcast, same_r[:, :], D_lo[:, :, :, :], start=False, stop=True)\
                        .then_inc(bcast_filled, 1)

            pe.wait_ge(small_loaded, 16 * SMALL_LOADS)
            pe.wait_ge(dve_setup, 9)
            pipeline(pe, iteration)

        @block.scalar
        def _(act):
            def split_weight(n):
                for c in range(DC):
                    act.wait_ge(w_loaded[n * DC + c], 16)
                    act.activation(w_hi[n][:, c, :], w_raw[n][:, c, :], ACT.Copy).then_inc(w_hi_ready, 1)

            def split_hT(k, p):
                act.wait_ge(hT_loaded, 16 * (k + 1))
                act.activation(hT_hi[p][:, :, :], hT[:, :, :], ACT.Copy).then_inc(hT_hi_ready, 1)

            split_weight(0)
            split_weight(1)
            split_weight(2)
            fill = 0
            for w in range(2):
                if w == 1:
                    split_weight(3)
                    split_hT(0, 0)
                for i in range(DC):
                    act.wait_ge(proj_filled, fill + 1)
                    act.activation(U_hi[w][:, tri(i, i):tri(i, i) + PART], ring[fill % RING][:, 0:PART],
                                   ACT.Copy, scale=0.5).then_inc(act_setup, 1)
                    if i < DC - 1:
                        act.activation(U_hi[w][:, tri(i, i) + PART:tri(i, i) + (DC - i) * PART],
                                       ring[fill % RING][:, PART:DIM - i * PART], ACT.Copy)\
                            .then_inc(act_setup, 1)
                    fill += 1
            for i in range(DC):
                act.wait_ge(proj_filled, fill + 1)
                act.activation(MT_hi[:, i, :], ring[fill % RING][:, :], ACT.Copy).then_inc(act_setup, 1)
                fill += 1
                if i == 0:
                    act.wait_ge(small_loaded, 16 * SMALL_LOADS)
                    act.activation(wtmp[:, 0:1], scal[:, 0:1], ACT.Exp, scale=-1.0).then_inc(exps_ready, 1)
                    act.activation(wtmp[:, 1:2], scal[:, 1:2], ACT.Exp, scale=-2.0).then_inc(exps_ready, 1)

            def take_hi(s, n, dst):
                act.wait_ge(proj_filled, FILLS * (s + 1) + n + 1)
                act.activation(dst, ring[n % RING][:, :], ACT.Copy).then_inc(proj_hi, 1)

            def norm_tile(n, t, dst, src, done):
                act.activation(dst, src, ACT.Identity, bias=shift[n][:, t:t + 1],
                               scale=rstd[n][:, t:t + 1]).then_inc(done, 1)

            def iteration(s, p):
                cur, prev, prev2 = live(s, 0), live(s, 1), live(s, 2)

                def h1_tile(t):
                    if prev:
                        if t == 0:
                            act.wait_ge(ln_step[0], 4 * s)
                        norm_tile(0, t, h1_hi[:, t, :], r[:, t, :], h1_ready)
                        norm_tile(0, t, r[:, t, :], r[:, t, :], h1_ready)

                def take_u(n):
                    if cur:
                        take_hi(s, n, UT_hi[:, n % DC, n // DC, :])

                def take_y(t):
                    if cur:
                        take_hi(s, 2 * DC + t, y_hi[:, t, :])

                def out_tile(t):
                    if prev2:
                        if t == 0:
                            act.wait_ge(ln_step[1], 4 * (s - 1))
                        norm_tile(1, t, o[:, t, :], o[:, t, :], out_ready)

                take_u(0)
                take_u(1)
                take_u(2)
                out_tile(0)
                out_tile(1)
                take_u(3)
                take_u(DC)
                if live(s, -1):
                    split_hT(s + 1, 1 - p)
                take_u(DC + 1)
                if prev:
                    act.wait_ge(kt_filled, s)
                    act.activation(KT_hi[:, :, :], KTp, ACT.Copy).then_inc(kt_hi_ready, 1)
                out_tile(2)
                take_u(DC + 2)
                out_tile(3)
                take_u(DC + 3)
                if cur:
                    act.wait_ge(gram_filled, s + 1)
                    act.activation(PT[:, :, :, :], lowp[:, :, :, :], ACT.Copy).then_inc(gram_taken, 1)
                h1_tile(0)
                h1_tile(1)
                take_y(0)
                h1_tile(2)
                h1_tile(3)
                take_y(1)
                take_y(2)
                if cur:
                    act.wait_ge(attn_step, ATTN_STEPS * s + DIAG_R)
                    act.activation(D_hi[:, :, :, :], D[:, :, :, :], ACT.Copy).then_inc(diag_hi_ready, 1)
                take_y(3)
                if cur:
                    act.wait_ge(attn_step, ATTN_STEPS * s + DIST)
                    act.activation(S[:, 1, :, :], S[:, 1, :, :], ACT.Exp, scale=neg_c[:, 0:1])\
                        .then_inc(exp_ready, 1)

            act.wait_ge(dve_setup, 9)
            pipeline(act, iteration)

        @block.vector
        def _(dve):
            def split_weight(n):
                for c in range(DC):
                    dve.wait_ge(w_hi_ready, n * DC + c + 1)
                    dve.tensor_tensor(w_lo[n][:, c, :], w_raw[n][:, c, :], w_hi[n][:, c, :].bitcast(fp32),
                                      ALU.subtract).then_inc(w_lo_ready, 1)

            split_weight(0)
            split_weight(1)
            split_weight(2)
            def small_constants():
                dve.wait_ge(small_loaded, 16 * SMALL_LOADS)
                dve.wait_ge(pool_setup, 3)
                dve.tensor_tensor(mask[:, :], adj2[:, :], eye, ALU.mult).then_inc(dve_setup, 1)
                dve.wait_ge(dve_setup, 1)
                dve.tensor_tensor(mask[:, :], adj2[:, :], mask[:, :], ALU.subtract).then_inc(dve_setup, 1)
                dve.tensor_tensor(adj2[:, :], adj2[:, :], adj2[:, :], ALU.mult).then_inc(dve_setup, 1)
                dve.wait_ge(dve_setup, 3)
                dve.tensor_copy(same_r[:, :], same)
                for g in range(2):
                    rows = slice(g * NODES, (g + 1) * NODES)
                    dve.tensor_tensor(W1[rows, rows], adj2[rows, :], cst[rows, 2 * PART:2 * PART + NODES],
                                      ALU.add).then_inc(dve_setup, 1)
                dve.wait_ge(dve_setup, 5)
                dve.tensor_copy(W1_hi[:, :], W1[:, :]).then_inc(dve_setup, 1)
                dve.wait_ge(dve_setup, 6)
                dve.tensor_tensor(W1_lo[:, :], W1[:, :], W1_hi[:, :].bitcast(fp32), ALU.subtract)\
                    .then_inc(dve_setup, 1)
                dve.wait_ge(exps_ready, 2)
                dve.tensor_scalar(neg_c[:, :], wtmp[:, 1:2], -0.5, None, ALU.mult).then_inc(dve_setup, 1)
                dve.tensor_scalar(wtmp[:, 2:3], wtmp[:, 0:1], 1.0, None, ALU.add).then_inc(dve_setup, 1)
                dve.wait_ge(dve_setup, 9)
                dve.reciprocal(wtmp[:, 3:4], wtmp[:, 2:3]).then_inc(dve_setup, 1)
                dve.wait_ge(dve_setup, 10)
                dve.tensor_copy(gain[:, 0, :], wtmp[:, 3:4].to_broadcast([PART, TPB])).then_inc(dve_setup, 1)
                dve.wait_ge(dve_setup, 11)
                dve.tensor_scalar(gain[:, 1, :], gain[:, 0, :], -1.0, 1.0, ALU.mult, ALU.add)\
                    .then_inc(dve_setup, 1)


            fill, taken = 0, 0
            for w in range(2):
                if w == 1:
                    split_weight(3)
                for i in range(DC):
                    taken += 1 + (i < DC - 1)
                    dve.wait_ge(act_setup, taken)
                    diag = slice(tri(i, i), tri(i, i) + PART)
                    last = dve.scalar_tensor_tensor(U_lo[w][:, diag], ring[fill % RING][:, 0:PART], 0.5,
                                                    U_hi[w][:, diag].bitcast(fp32), ALU.mult, ALU.subtract)
                    if i < DC - 1:
                        rest = slice(tri(i, i) + PART, tri(i, i) + (DC - i) * PART)
                        last = dve.tensor_tensor(U_lo[w][:, rest], ring[fill % RING][:, PART:DIM - i * PART],
                                                 U_hi[w][:, rest].bitcast(fp32), ALU.subtract)
                    last.then_inc(proj_lo, 1)
                    fill += 1
            for i in range(DC):
                taken += 1
                dve.wait_ge(act_setup, taken)
                dve.tensor_tensor(MT_lo[:, i, :], ring[fill % RING][:, :], MT_hi[:, i, :].bitcast(fp32),
                                  ALU.subtract).then_inc(proj_lo, 1)
                fill += 1
                if i == 0:
                    small_constants()

            def take_lo(s, n, dst, hi):
                dve.wait_ge(proj_hi, FILLS * s + n + 1)
                dve.tensor_tensor(dst, ring[n % RING][:, :], hi.bitcast(fp32), ALU.subtract)\
                    .then_inc(proj_lo, 1)

            eye_b = eye.unsqueeze(1).to_broadcast([PART, 2 * TPB, NODES])
            eye_t = eye.unsqueeze(1).to_broadcast([PART, TPB, NODES])
            mask_t = mask[:, :].unsqueeze(1).to_broadcast([PART, TPB, NODES])

            def over_cols(v):
                return v.unsqueeze(2).to_broadcast([PART, v.shape[1], NODES])

            S_all = S[:, :, :, :].rearrange("p w t n -> p (w t) n")
            D_all = D[:, :, :, :].rearrange("p w t n -> p (w t) n")
            sq_all = sq[:, :, :].rearrange("p w t -> p (w t)")
            deg_all = deg[:, :, :].rearrange("p w t -> p (w t)")
            gain_all = gain[:, :, :].rearrange("p w t -> p (w t)")

            def iteration(s, p):
                cur, prev, prev2 = live(s, 0), live(s, 1), live(s, 2)

                def attn(k, step):
                    dve.wait_ge(attn_step, ATTN_STEPS * k + step)

                def take_u(n):
                    if cur:
                        take_lo(s, n, UT_lo[:, n % DC, n // DC, :], UT_hi[:, n % DC, n // DC, :])

                def take_y(t):
                    if cur:
                        take_lo(s, 2 * DC + t, y_lo[:, t, :], y_hi[:, t, :])

                def statistics(n, t, src):
                    dve.bn_stats(st[n][:, t, :], src).then_inc(stat[n], 1)

                def aggregate(n):
                    for t in range(TPB):
                        dve.bn_aggr(mv[n][:, t, :], st[n][:, t, :]).then_inc(stat[n], 1)

                def residual(t):
                    if prev:
                        if t == 0:
                            dve.wait_ge(h_loaded, 16 * s)
                        dve.wait_ge(ky_filled, TPB * (s - 1) + t + 1)
                        dve.tensor_tensor(r[:, t, :], high2[:, t % 2, :], h[:, t, :], ALU.add)\
                            .then_inc(ky_taken, 1)

                def residual_statistics(t):
                    if prev:
                        dve.wait_ge(ky_taken, TPB * (s - 1) + t + 1)
                        statistics(0, t, r[:, t, :])

                def add_bias(t):
                    if prev:
                        if t == 0:
                            ge(dve, out_stored, 16 * (s - 1))
                        dve.wait_ge(mix_filled, TPB * (s - 1) + t + 1)
                        dve.tensor_tensor(o[:, t, :], mix_bank[t], bias_b[:, :], ALU.add)\
                            .then_inc(mix_taken, 1)

                def out_statistics(t):
                    if prev:
                        dve.wait_ge(mix_taken, TPB * (s - 1) + t + 1)
                        statistics(1, t, o[:, t, :])

                if prev2:
                    dve.wait_ge(stat[1], 2 * TPB * (s - 2) + TPB)
                take_u(0)
                if prev2:
                    aggregate(1)
                take_u(1)
                if prev:
                    attn(s - 1, COS)
                    dve.scalar_tensor_tensor(S[:, 0, :, :], S[:, 0, :, :], 0.0, mask_t, ALU.max, ALU.mult)\
                        .then_inc(attn_step, 1)
                    dve.wait_ge(exp_ready, s)
                    dve.scalar_tensor_tensor(S[:, 1, :, :], S[:, 1, :, :], 1.0, mask_t, ALU.min, ALU.mult)\
                        .then_inc(attn_step, 1)
                    attn(s - 1, A_GRAV)
                    dve.reduce_sum(deg_all, S_all, AX.X).then_inc(attn_step, 1)
                    attn(s - 1, DEG)
                    dve.tensor_scalar(deg_all, deg_all, EPS, None, ALU.max).then_inc(attn_step, 1)
                    attn(s - 1, DEG_MAX)
                    dve.reciprocal(deg_all, deg_all).then_inc(attn_step, 1)
                    attn(s - 1, DEG_INV)
                    dve.tensor_tensor(deg_all, deg_all, gain_all, ALU.mult).then_inc(attn_step, 1)
                    attn(s - 1, FACTOR)
                    dve.tensor_tensor(S_all, S_all, over_cols(deg_all), ALU.mult).then_inc(attn_step, 1)
                    attn(s - 1, SCALED)
                    for g in range(2):
                        rows = slice(g * NODES, (g + 1) * NODES)
                        dve.tensor_tensor(K[rows, :, rows], S[rows, 0, :, :], S[rows, 1, :, :], ALU.add)\
                            .then_inc(attn_step, 1)
                for n in range(2, DC + 2):
                    take_u(n)
                if prev:
                    dve.wait_ge(kt_hi_ready, s)
                    dve.tensor_tensor(KT_lo[:, :, :], KTp, KT_hi[:, :, :].bitcast(fp32), ALU.subtract)\
                        .then_inc(kt_lo_ready, 1)
                take_u(DC + 2)
                take_u(DC + 3)
                residual(0)
                residual(1)
                residual_statistics(0)
                residual_statistics(1)
                residual(2)
                residual_statistics(2)
                residual(3)
                residual_statistics(3)
                if prev:
                    dve.wait_ge(stat[0], 2 * TPB * (s - 1) + TPB)
                    dve.memset(anchor[:, :], 0.0)
                    aggregate(0)
                take_y(0)
                if cur:
                    dve.wait_ge(pt_filled, s + 1)
                    for g in range(2):
                        rows = slice(g * NODES, (g + 1) * NODES)
                        dve.tensor_tensor(S[rows, :, :, :].rearrange("p w t n -> p t w n"),
                                          highp[rows, :, :, rows], PT[rows, :, :, rows], ALU.add)\
                            .then_inc(attn_step, 1)
                    attn(s, SUM_B)
                    dve.tensor_tensor(D_all, S_all, eye_b, ALU.mult).then_inc(attn_step, 1)
                    attn(s, DIAG)
                    dve.reduce_sum(sq_all, D_all, AX.X).then_inc(attn_step, 1)
                    attn(s, SQ)
                    dve.tensor_scalar(rq[:, :], sq[:, 0, :], EPS * EPS, None, ALU.max)\
                        .then_inc(attn_step, 1)
                    dve.scalar_tensor_tensor(S[:, 1, :, :], S[:, 1, :, :], -2.0, over_cols(sq[:, 1, :]),
                                             ALU.mult, ALU.add).then_inc(attn_step, 1)
                take_y(1)
                add_bias(0)
                add_bias(1)
                take_y(2)
                if cur:
                    dve.wait_ge(rnorm_ready, s + 1)
                    dve.tensor_tensor(D[:, 0, :, :], eye_t, over_cols(rn[:, :]), ALU.mult)\
                        .then_inc(attn_step, 1)
                    dve.tensor_tensor(S[:, 0, :, :], S[:, 0, :, :], over_cols(rn[:, :]), ALU.mult)\
                        .then_inc(attn_step, 1)
                add_bias(2)
                if cur:
                    dve.wait_ge(diag_hi_ready, s + 1)
                    dve.tensor_tensor(D_lo[:, :, :, :], D[:, :, :, :], D_hi[:, :, :, :].bitcast(fp32),
                                      ALU.subtract).then_inc(attn_step, 1)
                add_bias(3)
                out_statistics(0)
                out_statistics(1)
                take_y(3)
                if cur:
                    dve.wait_ge(bcast_filled, s + 1)
                    attn(s, COS_ROWS)
                    dve.tensor_tensor(S[:, 1, :, :], bcast[:, 1, :, :], S[:, 1, :, :], ALU.add)\
                        .then_inc(attn_step, 1)
                    dve.tensor_tensor(S[:, 0, :, :], bcast[:, 0, :, :], S[:, 0, :, :], ALU.mult)\
                        .then_inc(attn_step, 1)
                out_statistics(2)
                out_statistics(3)

            pipeline(dve, iteration)

        @block.gpsimd
        def _(pool):
            pool.memset(W1[:, :], 0.0).then_inc(pool_setup, 1)
            pool.memset(K[:, :, :], 0.0).then_inc(pool_setup, 1)
            pool.memset(minus_half[:, :], -0.5).then_inc(pool_setup, 1)
            pool.memset(minus_one[:, :], -1.0).then_inc(pool_setup, 1)
            pool.memset(ln_eps[:, :], LN_EPS).then_inc(pool_setup, 1)
            pool.wait_ge(pool_setup, 5)

            def split_hT(k, p):
                pool.wait_ge(hT_hi_ready, k + 1)
                pool.tensor_tensor(hT_lo[p][:, :, :], hT[:, :, :], hT_hi[p][:, :, :].bitcast(fp32),
                                   ALU.subtract).then_inc(hT_lo_ready, 1)

            def norm_factors(n, k):
                pool.wait_ge(stat[n], 2 * TPB * (k + 1))
                pool.tensor_tensor(var_e[n][:, :], mv[n][:, :, 1], ln_eps[:, :], ALU.add)\
                    .then_inc(ln_step[n], 1)
                pool.tensor_tensor(neg_m[n][:, :], mv[n][:, :, 0], minus_one[:, :], ALU.mult)\
                    .then_inc(ln_step[n], 1)
                pool.wait_ge(ln_step[n], 4 * k + 2)
                pool.tensor_tensor(rstd[n][:, :], var_e[n][:, :], minus_half[:, :], ALU.pow)\
                    .then_inc(ln_step[n], 1)
                pool.wait_ge(ln_step[n], 4 * k + 3)
                pool.tensor_tensor(shift[n][:, :], neg_m[n][:, :], rstd[n][:, :], ALU.mult)\
                    .then_inc(ln_step[n], 1)

            def iteration(s, p):
                cur, prev, prev2 = live(s, 0), live(s, 1), live(s, 2)

                def h1_rest(t):
                    if prev:
                        pool.wait_ge(h1_ready, 2 * (TPB * (s - 1) + t + 1))
                        pool.tensor_tensor(h1_lo[:, t, :], r[:, t, :], h1_hi[:, t, :].bitcast(fp32),
                                           ALU.subtract).then_inc(h1_lo_ready, 1)

                if prev2:
                    norm_factors(1, s - 2)
                if live(s, -1):
                    split_hT(s + 1, 1 - p)
                if prev:
                    norm_factors(0, s - 1)
                for t in range(TPB):
                    h1_rest(t)
                if cur:
                    pool.wait_ge(attn_step, ATTN_STEPS * s + SQ_MAX)
                    pool.tensor_tensor(rn[:, :], rq[:, :], minus_half[:, :], ALU.pow)\
                        .then_inc(rnorm_ready, 1)

            split_hT(0, 0)
            pipeline(pool, iteration)


def kernel(x, adj, L0_gnn_W_lang, L0_gnn_W_grav, L0_gnn_W_V, L0_gnn_W_O, L0_gnn_gate_logit,
           L0_gnn_log_sigma, L1_gnn_bias):
    import numpy as np
    import concourse.bacc as bacc
    from concourse.bass_utils import run_bass_kernel_spmd

    x = np.ascontiguousarray(x).reshape(TOKENS, DIM)
    same = np.zeros((PART, PART), np.float32)
    for g in range(PART // NODES):
        same[g * NODES:(g + 1) * NODES, g * NODES:(g + 1) * NODES] = 1.0
    arrays = {
        "x": x,
        "xT": np.ascontiguousarray(x.reshape(NB, BLOCK, DC, PART).transpose(0, 3, 2, 1)),
        "adj": np.ascontiguousarray(adj),
        "w_lang": np.ascontiguousarray(L0_gnn_W_lang),
        "w_grav": np.ascontiguousarray(L0_gnn_W_grav),
        "w_v": np.ascontiguousarray(L0_gnn_W_V),
        "w_oT": np.ascontiguousarray(np.asarray(L0_gnn_W_O).T),
        "gate": np.asarray(L0_gnn_gate_logit).reshape(1, 1),
        "log_sigma": np.asarray(L0_gnn_log_sigma).reshape(1, 1),
        "bias": np.ascontiguousarray(L1_gnn_bias).reshape(1, DIM),
        "consts": np.concatenate(
            [np.eye(PART, dtype=np.float32), same,
             np.concatenate([np.eye(NODES, dtype=np.float32)] * (PART // NODES))], axis=1),
    }
    nc = bacc.Bacc("TRN2", target_bir_lowering=False, num_devices=1)
    aps = {n: nc.dram_tensor(n, a.shape, mybir.dt.from_np(a.dtype), kind="ExternalInput").ap()
           for n, a in arrays.items()}
    aps["out"] = nc.dram_tensor("out", (TOKENS, DIM), mybir.dt.float32, kind="ExternalOutput").ap()
    build(nc, **aps)
    res = run_bass_kernel_spmd(nc, [arrays], core_ids=[0])
    return res.results[0]["out"].reshape(GRAPHS, NODES, DIM)
```

```python
from contextlib import ExitStack

import concourse.bass as bass
from concourse import mybir

GRAPHS, NODES, DIM = 128, 64, 512
PART = 128
TOKENS = GRAPHS * NODES
BLOCK = 512
NB = TOKENS // BLOCK
TPB = BLOCK // PART
DC = DIM // PART
TRI = DC * (DC + 1) // 2
FILLS = 2 * DC + TPB
RING = 4
SQUARE = 32
QUADRANTS = PART // SQUARE
WARM_UP = 8
EPS = 1e-8
LN_EPS = 1e-5

STEPS = ("TURN_A TURN_B SUM_1 SUM_2 SUM_3 SUM_4 SUM_5 SUM_6 SUM_7 SUM DIAG SQ SQ_MAX GRAV_ROWS "
         "SCALE_TURNED COS_ROWS DIST COS A_LANG A_GRAV DEG DEG_MAX DEG_INV FACTOR SCALED K_SUM K_TURNED").split()
ATTN_STEPS = len(STEPS)
(TURN_B, SUM, DIAG, SQ, SQ_MAX, GRAV_ROWS, SCALE_TURNED, COS_ROWS, DIST, COS, A_GRAV, DEG, DEG_MAX,
 DEG_INV, FACTOR, SCALED, K_SUM, K_TURNED) = (STEPS.index(name) + 1 for name in (
     "TURN_B SUM DIAG SQ SQ_MAX GRAV_ROWS SCALE_TURNED COS_ROWS DIST COS A_GRAV DEG DEG_MAX DEG_INV "
     "FACTOR SCALED K_SUM K_TURNED").split())


def tri(i, j):
    return (i * DC - i * (i - 1) // 2 + (j - i)) * PART


def build(nc, x, xT, adj, w_lang, w_grav, w_v, w_oT, gate, log_sigma, bias, eyes, out):
    fp32, fp32r = mybir.dt.float32, mybir.dt.float32r
    ALU, ACT, AX = mybir.AluOpType, mybir.ActivationFunctionType, mybir.AxisListType

    x_blk = x.rearrange("(s t p) d -> s p t d", t=TPB, p=PART)
    out_blk = out.rearrange("(s t p) d -> s p t d", t=TPB, p=PART)

    with ExitStack() as ctx:
        def sb(name, shape, dt=fp32):
            return ctx.enter_context(nc.sbuf_tensor(name, shape, dt))

        def sem(name):
            return ctx.enter_context(nc.semaphore(name))

        h = sb("h", [PART, TPB, DIM])
        hT = sb("hT", [PART, DC, BLOCK])
        hT_hi = [sb(f"hT_hi{p}", [PART, DC, BLOCK], fp32r) for p in range(2)]
        hT_lo = [sb(f"hT_lo{p}", [PART, DC, BLOCK], fp32r) for p in range(2)]
        UT_hi = sb("UT_hi", [PART, DC, 2, BLOCK], fp32r)
        UT_lo = sb("UT_lo", [PART, DC, 2, BLOCK], fp32r)
        y_hi = sb("y_hi", [PART, TPB, DIM], fp32r)
        y_lo = sb("y_lo", [PART, TPB, DIM], fp32r)
        U_hi = [sb(f"U_hi{w}", [PART, TRI * PART], fp32r) for w in range(2)]
        U_lo = [sb(f"U_lo{w}", [PART, TRI * PART], fp32r) for w in range(2)]
        MT_hi = sb("MT_hi", [PART, DC, DIM], fp32r)
        MT_lo = sb("MT_lo", [PART, DC, DIM], fp32r)
        turned = sb("turned", [PART, TPB, 2, NODES])
        S = sb("S", [PART, 2, TPB, NODES])
        D = sb("D", [PART, 2, TPB, NODES])
        scale_turned = sb("scale_turned", [PART, 2, TPB, SQUARE])
        scale_cols = sb("scale_cols", [PART, 2, TPB, NODES])
        K = sb("K", [PART, TPB, NODES])
        K_turned = sb("K_turned", [PART, TPB, NODES])
        KT = sb("KT", [PART, TPB, PART])
        KT_hi = sb("KT_hi", [PART, TPB, PART], fp32r)
        KT_lo = sb("KT_lo", [PART, TPB, PART], fp32r)
        r = sb("r", [PART, TPB, DIM])
        h1_hi = sb("h1_hi", [PART, TPB, DIM], fp32r)
        h1_lo = sb("h1_lo", [PART, TPB, DIM], fp32r)
        o = sb("o", [PART, TPB, DIM])
        w_stage = sb("w_stage", [PART, DC, DIM])
        h1_full = w_stage
        y_last = hT
        o_last = hT
        W1 = sb("W1", [PART, PART])
        W1_hi = sb("W1_hi", [PART, PART], fp32r)
        W1_lo = sb("W1_lo", [PART, PART], fp32r)
        eye = sb("eye", [PART, NODES])
        adj2 = sb("adj2", [PART, NODES])
        mask = sb("mask", [PART, NODES])
        bias_b = sb("bias_b", [PART, DIM])
        bias_hi = sb("bias_hi", [1, DIM], fp32r)
        bias_lo = sb("bias_lo", [1, DIM], fp32r)
        ones = sb("ones", [1, PART], fp32r)
        scal = sb("scal", [PART, 2])
        gain = sb("gain", [PART, 2, TPB])
        wtmp = sb("wtmp", [PART, 4])
        neg_c = sb("neg_c", [PART, 1])
        scale = sb("scale", [PART, 2, TPB])
        sq_max = sb("sq_max", [PART, TPB])
        deg = sb("deg", [PART, 2, TPB])
        anchor = sb("anchor", [PART, 1])
        minus_half = sb("minus_half", [PART, TPB])
        minus_one = sb("minus_one", [PART, TPB])
        ln_eps = sb("ln_eps", [PART, TPB])
        st = [sb(f"st{n}", [PART, TPB, 6]) for n in range(2)]
        mv = [sb(f"mv{n}", [PART, TPB, 2]) for n in range(2)]
        var_e = [sb(f"var_e{n}", [PART, TPB]) for n in range(2)]
        rstd = [sb(f"rstd{n}", [PART, TPB]) for n in range(2)]
        neg_m = [sb(f"neg_m{n}", [PART, TPB]) for n in range(2)]
        shift = [sb(f"shift{n}", [PART, TPB]) for n in range(2)]

        ring = [ctx.enter_context(nc.psum_tensor(f"ring{b}", [PART, BLOCK], fp32))
                for b in range(RING)]
        lowp = ctx.enter_context(nc.psum_tensor("lowp", [PART, TPB, 2, PART], fp32))
        highp = ctx.enter_context(nc.psum_tensor("highp", [PART, 2, BLOCK], fp32))
        low2 = lowp[:, :, :, :].rearrange("p (b t) w n -> p b (t w n)", b=2)
        high2 = highp[:, :, :]
        mix_bank = [low2[:, 0, :], low2[:, 1, :], high2[:, 0, :], high2[:, 1, :]]

        w_loaded = [sem(f"w_loaded{n}") for n in range(4 * DC)]
        small_loaded = sem("small_loaded")
        hT_loaded = sem("hT_loaded")
        h_loaded = sem("h_loaded")
        out_stored = sem("out_stored")
        w_hi_ready = sem("w_hi_ready")
        w_lo_ready = sem("w_lo_ready")
        act_setup = sem("act_setup")
        exps_ready = sem("exps_ready")
        dve_setup = sem("dve_setup")
        pool_setup = sem("pool_setup")
        hT_hi_ready = sem("hT_hi_ready")
        hT_lo_ready = sem("hT_lo_ready")
        proj_filled = sem("proj_filled")
        proj_hi = sem("proj_hi")
        proj_lo = sem("proj_lo")
        gram_filled = sem("gram_filled")
        attn_step = sem("attn_step")
        scale_own = sem("scale_own")
        scale_off = sem("scale_off")
        rnorm_ready = sem("rnorm_ready")
        exp_ready = sem("exp_ready")
        kt_diag = sem("kt_diag")
        kt_off = sem("kt_off")
        kt_hi_ready = sem("kt_hi_ready")
        kt_lo_ready = sem("kt_lo_ready")
        ky_filled = sem("ky_filled")
        ky_taken = sem("ky_taken")
        stat = [sem(f"stat{n}") for n in range(2)]
        ln_step = [sem(f"ln_step{n}") for n in range(2)]
        h1_ready = sem("h1_ready")
        h1_lo_ready = sem("h1_lo_ready")
        mix_filled = sem("mix_filled")
        mix_taken = sem("mix_taken")
        out_ready = sem("out_ready")
        h1_full_dve = sem("h1_full_dve")
        h1_lo_dve = sem("h1_lo_dve")
        out_ready_dve = sem("out_ready_dve")
        mix_copied = sem("mix_copied")
        mix_biased = sem("mix_biased")
        y_copied = sem("y_copied")
        y_lo_pool = sem("y_lo_pool")

        SMALL_LOADS = 6
        w_raw = [r, o, h, w_stage]
        w_hi = [UT_hi[:, :, 0, :], UT_hi[:, :, 1, :], y_hi[:, :, :], h1_hi[:, :, :]]
        w_lo = [UT_lo[:, :, 0, :], UT_lo[:, :, 1, :], y_lo[:, :, :], h1_lo[:, :, :]]

        def ge(eng, semaphore, value):
            if not isinstance(value, int) or value > 0:
                eng.wait_ge(semaphore, value)

        def live(s, back):
            return not isinstance(s, int) or 0 <= s - back < NB

        def pipeline(eng, iteration):
            iteration(0, 0)
            iteration(1, 1)
            with eng.Fori(1, NB // 2 - 1) as i:
                iteration(2 * i, 0)
                iteration(2 * i + 1, 1)
            for s in range(NB - 2, NB + 2):
                iteration(s, s % 2)

        def fills_before(s, n):
            late = DC if isinstance(s, int) and s == 0 and n < 2 * DC else 0
            return FILLS * (s + 1) + n - late

        def kt_square(q, m):
            dst = KT[q * SQUARE:(q + 1) * SQUARE, :, m * SQUARE:(m + 1) * SQUARE]
            src = K_turned[m * SQUARE:(m + 1) * SQUARE, :, q % 2 * SQUARE:(q % 2 + 1) * SQUARE]
            return dst, src

        def scale_square(q, m):
            dst = scale_cols[q * SQUARE:(q + 1) * SQUARE, :, :, m % 2 * SQUARE:(m % 2 + 1) * SQUARE]
            return dst, scale_turned[m * SQUARE:(m + 1) * SQUARE, :, :, :]

        def is_last(k):
            return isinstance(k, int) and k == NB - 1

        HALF = TPB // 2
        LAST_H1 = 2 * TPB * (NB - 1)
        block = ctx.enter_context(nc.Block())

        @block.sync
        def _(sp):
            def load_weight(n, w):
                for c in range(DC):
                    sp.dma_start(w_raw[n][:, c, :], w[c * PART:(c + 1) * PART, :])\
                        .then_inc(w_loaded[n * DC + c], 16)

            load_weight(0, w_lang)
            load_weight(1, w_grav)
            load_weight(2, w_v)
            sp.dma_start(hT[:, :, :], xT[0]).then_inc(hT_loaded, 16)
            load_weight(3, w_oT)
            sp.dma_start(eye[:, :], eyes).then_inc(small_loaded, 16)
            for g in range(2):
                sp.dma_start(adj2[g * NODES:(g + 1) * NODES, :], adj).then_inc(small_loaded, 16)
            sp.dma_start(bias_b[:, :], bias.to_broadcast([PART, DIM])).then_inc(small_loaded, 16)
            sp.dma_start(scal[:, 0:1], gate.to_broadcast([PART, 1])).then_inc(small_loaded, 16)
            sp.dma_start(scal[:, 1:2], log_sigma.to_broadcast([PART, 1])).then_inc(small_loaded, 16)
            sp.wait_ge(hT_lo_ready, 1)
            sp.dma_start(hT[:, :, :], xT[1]).then_inc(hT_loaded, 16)

            def iteration(s, p):
                if live(s, 2) and is_last(s - 2):
                    for t in range(TPB):
                        if t < TPB - 1:
                            sp.wait_ge(out_ready, TPB * (s - 2) + t + 1)
                        else:
                            sp.wait_ge(out_ready_dve, 1)
                        sp.dma_start(out_blk[s - 2, :, t, :], o_last[:, t, :]).then_inc(out_stored, 16)
                elif live(s, 2):
                    sp.wait_ge(out_ready, TPB * (s - 1))
                    sp.dma_start(out_blk[s - 2], o[:, :, :]).then_inc(out_stored, 16)
                if live(s, -2):
                    sp.wait_ge(hT_lo_ready, s + 2)
                    sp.dma_start(hT[:, :, :], xT[s + 2]).then_inc(hT_loaded, 16)
                if live(s, 0):
                    if isinstance(s, int) and s == 0:
                        sp.wait_ge(w_lo_ready, 3 * DC)
                    else:
                        sp.wait_ge(ky_taken, TPB * s)
                    sp.dma_start(h[:, :, :], x_blk[s]).then_inc(h_loaded, 16)

            pipeline(sp, iteration)
            sp.wait_ge(out_stored, 16 * (NB - 1 + TPB))

        @block.tensor
        def _(pe):
            def three_pass(dst, terms, done, start=True, stop=True):
                last = None
                for n, (a_hi, a_lo, b_hi, b_lo) in enumerate(terms):
                    pe.matmul(dst, a_hi, b_hi, start=(start and n == 0), stop=False)
                    pe.matmul(dst, a_hi, b_lo, start=False, stop=False)
                    last = pe.matmul(dst, a_lo, b_hi, start=False, stop=(stop and n == len(terms) - 1))
                if done is not None:
                    last.then_inc(done, 1)

            pe.wait_ge(pool_setup, 2)
            for n in range(WARM_UP):
                pe.matmul(ring[0][:, 0:PART], KT[:, 0, :], KT[:, 0, :], start=True, stop=True)

            fill = 0
            for k in range(DC):
                pe.wait_ge(w_lo_ready, k + 1)
                for i in range(DC):
                    sl = slice(i * PART, (i + 1) * PART)
                    three_pass(ring[i][:, 0:DIM - i * PART],
                               [(UT_hi[:, k, 0, sl], UT_lo[:, k, 0, sl],
                                 UT_hi[:, k, 0, i * PART:], UT_lo[:, k, 0, i * PART:])],
                               proj_filled if k == DC - 1 else None, start=(k == 0), stop=(k == DC - 1))
            fill = DC
            for w in range(1, 2):
                for i in range(DC):
                    ge(pe, proj_lo, fill - RING + 1)
                    terms = []
                    for k in range(DC):
                        sl = slice(i * PART, (i + 1) * PART)
                        terms.append((UT_hi[:, k, w, sl], UT_lo[:, k, w, sl],
                                      UT_hi[:, k, w, i * PART:], UT_lo[:, k, w, i * PART:]))
                    if i == 0:
                        pe.wait_ge(w_lo_ready, DC * (w + 1))
                    three_pass(ring[fill % RING][:, 0:DIM - i * PART], terms, proj_filled)
                    fill += 1
            def value_weights():
                pe.wait_ge(w_lo_ready, 4 * DC)
                for i in range(DC):
                    pe.wait_ge(proj_lo, 4 * DC + i - RING + 1)
                    sl = slice(i * PART, (i + 1) * PART)
                    three_pass(ring[i % RING][:, :],
                               [(y_hi[:, k, sl], y_lo[:, k, sl], h1_hi[:, k, :], h1_lo[:, k, :])
                                for k in range(DC)], proj_filled)

            def project(s, p, w, j):
                n = w * DC + j
                ge(pe, proj_lo, fills_before(s, n) - RING + 1)
                three_pass(ring[n % RING][:, :],
                           [(U_hi[w][:, tri(i, j):tri(i, j) + PART], U_lo[w][:, tri(i, j):tri(i, j) + PART],
                             hT_hi[p][:, i, :], hT_lo[p][:, i, :]) for i in range(j + 1)], proj_filled)

            def value_tile(s, p, t):
                if isinstance(s, int) and s == 0 and t == 0:
                    pe.wait_ge(proj_lo, 5 * DC)
                n = 2 * DC + t
                ge(pe, proj_lo, fills_before(s, n) - RING + 1)
                sl = slice(t * PART, (t + 1) * PART)
                three_pass(ring[n % RING][:, :],
                           [(hT_hi[p][:, c, sl], hT_lo[p][:, c, sl], MT_hi[:, c, :], MT_lo[:, c, :])
                            for c in range(DC)], proj_filled)

            def gram_tile(s, p, t):
                sl = slice(t * PART, (t + 1) * PART)
                terms = [(hT_hi[p][:, j, sl], hT_lo[p][:, j, sl], UT_hi[:, j, :, sl], UT_lo[:, j, :, sl])
                         for j in range(DC)]
                if t == 0:
                    pe.wait_ge(proj_lo, fills_before(s, 2 * DC - 1))
                three_pass(lowp[:, t, :, :], terms[:-1], None, stop=False)
                if t == 0:
                    pe.wait_ge(proj_lo, fills_before(s, 2 * DC - 1) + 1)
                three_pass(lowp[:, t, :, :], terms[-1:], gram_filled if t == TPB - 1 else None, start=False)

            def attend_tile(k, t):
                if t == 0:
                    pe.wait_ge(kt_lo_ready, k + 1)
                    if not is_last(k):
                        ge(pe, mix_taken, TPB * k)
                if is_last(k) and t < 2:
                    pe.wait_ge(mix_copied, t + 2)
                if t >= 2:
                    pe.wait_ge(ky_taken, TPB * k + t - 1)
                if is_last(k) and t >= 1:
                    pe.wait_ge(y_lo_pool, t)
                three_pass(high2[:, t % 2, :],
                           [(KT_hi[:, t, :], KT_lo[:, t, :], y_hi[:, t, :], y_lo[:, t, :])], ky_filled)

            def mix_tile(k, t):
                if is_last(k):
                    pe.wait_ge(h1_lo_dve, t + 1)
                else:
                    pe.wait_ge(h1_lo_ready, TPB * k + t + 1)
                three_pass(mix_bank[t],
                           [(W1_hi[:, :], W1_lo[:, :], h1_hi[:, t, :], h1_lo[:, t, :])], mix_filled,
                           start=not is_last(k))

            def iteration(s, p):
                cur, prev = live(s, 0), live(s, 1)
                if cur:
                    pe.wait_ge(hT_lo_ready, s + 1)
                    for j in range(DC):
                        project(s, p, 0, j)
                    project(s, p, 1, 0)
                    project(s, p, 1, 1)
                    project(s, p, 1, 2)
                    project(s, p, 1, 3)
                if isinstance(s, int) and s == 0:
                    value_weights()
                    pe.wait_ge(dve_setup, 8)
                if prev:
                    attend_tile(s - 1, 0)
                    attend_tile(s - 1, 1)
                if cur:
                    gram_tile(s, p, 0)
                if prev:
                    attend_tile(s - 1, 2)
                if cur:
                    gram_tile(s, p, 1)
                if prev:
                    attend_tile(s - 1, 3)
                if cur:
                    gram_tile(s, p, 2)
                    gram_tile(s, p, 3)
                if is_last(s):
                    value_tile(s, p, 0)
                    value_tile(s, p, 1)
                    pe.wait_ge(attn_step, ATTN_STEPS * s + SUM)
                    mix_tile(s - 1, 0)
                    mix_tile(s - 1, 1)
                    value_tile(s, p, 2)
                    mix_tile(s - 1, 2)
                    mix_tile(s - 1, 3)
                    value_tile(s, p, 3)
                elif is_last(s - 1):
                    pe.wait_ge(mix_taken, TPB * (s - 2) + 1)
                    pe.wait_ge(mix_copied, 1)
                    for t in range(TPB):
                        if t >= 2:
                            pe.wait_ge(ky_taken, TPB * (s - 1) + t + 1)
                        pe.matmul(mix_bank[t], ones[:, :], bias_hi[:, :], start=True, stop=False)
                        pe.matmul(mix_bank[t], ones[:, :], bias_lo[:, :], start=False, stop=False)
                    for t in range(TPB):
                        mix_tile(s - 1, t)
                elif cur:
                    value_tile(s, p, 0)
                    value_tile(s, p, 1)
                    if prev:
                        pe.wait_ge(attn_step, ATTN_STEPS * s + SUM)
                        mix_tile(s - 1, 0)
                        mix_tile(s - 1, 1)
                    value_tile(s, p, 2)
                    if prev:
                        mix_tile(s - 1, 2)
                        mix_tile(s - 1, 3)
                    value_tile(s, p, 3)

            pipeline(pe, iteration)

        @block.scalar
        def _(act):
            def split_weight(n):
                for c in range(DC):
                    act.wait_ge(w_loaded[n * DC + c], 16)
                    act.activation(w_hi[n][:, c, :], w_raw[n][:, c, :], ACT.Copy).then_inc(w_hi_ready, 1)

            def split_hT(k, p):
                act.wait_ge(hT_loaded, 16 * (k + 1))
                act.activation(hT_hi[p][:, :, :], hT[:, :, :], ACT.Copy).then_inc(hT_hi_ready, 1)

            split_weight(0)
            split_weight(1)
            split_weight(2)
            fill = 0
            for w in range(2):
                if w == 1:
                    split_hT(0, 0)
                    split_weight(3)
                for i in range(DC):
                    act.wait_ge(proj_filled, fill + 1)
                    act.activation(U_hi[w][:, tri(i, i):tri(i, i) + PART], ring[fill % RING][:, 0:PART],
                                   ACT.Copy, scale=0.5).then_inc(act_setup, 1)
                    if i < DC - 1:
                        act.activation(U_hi[w][:, tri(i, i) + PART:tri(i, i) + (DC - i) * PART],
                                       ring[fill % RING][:, PART:DIM - i * PART], ACT.Copy)\
                            .then_inc(act_setup, 1)
                    fill += 1
            act.wait_ge(small_loaded, 16 * SMALL_LOADS)
            act.activation(wtmp[:, 0:1], scal[:, 0:1], ACT.Exp, scale=-1.0).then_inc(exps_ready, 1)
            act.activation(wtmp[:, 1:2], scal[:, 1:2], ACT.Exp, scale=-2.0).then_inc(exps_ready, 1)

            def take_hi(s, n, dst):
                act.wait_ge(proj_filled, fills_before(s, n) + 1)
                act.activation(dst, ring[n % RING][:, :], ACT.Copy).then_inc(proj_hi, 1)

            def take_last_y(k, t):
                n = 2 * DC + t
                take_hi(k, n, y_hi[:, t, :])
                act.activation(y_last[:, t, :], ring[n % RING][:, :], ACT.Copy).then_inc(y_copied, 1)

            def norm_tile(n, t, dst, src, done):
                act.activation(dst, src, ACT.Identity, bias=shift[n][:, t:t + 1],
                               scale=rstd[n][:, t:t + 1]).then_inc(done, 1)

            def iteration(s, p):
                cur, prev, prev2 = live(s, 0), live(s, 1), live(s, 2)

                def h1_hi_tile(t):
                    norm_tile(0, t, h1_hi[:, t, :], r[:, t, :], h1_ready)

                def h1_tile(t):
                    if prev:
                        if t == 0:
                            act.wait_ge(ln_step[0], 4 * s)
                        h1_hi_tile(t)
                        norm_tile(0, t, r[:, t, :], r[:, t, :], h1_ready)

                def take_u(n):
                    if cur:
                        take_hi(s, n, UT_hi[:, n % DC, n // DC, :])

                def take_y(t):
                    if cur:
                        take_hi(s, 2 * DC + t, y_hi[:, t, :])

                def out_tile(t):
                    if prev2 and is_last(s - 2):
                        if t % HALF == 0:
                            act.wait_ge(ln_step[1], 4 * (s - 2) + 4 * (t // HALF + 1))
                        if t < TPB - 1:
                            norm_tile(1, t, o_last[:, t, :], mix_bank[t], out_ready)
                    elif prev2:
                        if t == 0:
                            act.wait_ge(ln_step[1], 4 * (s - 1))
                        norm_tile(1, t, o[:, t, :], o[:, t, :], out_ready)

                take_u(0)
                take_u(1)
                take_u(2)
                if prev:
                    act.wait_ge(attn_step, ATTN_STEPS * (s - 1) + K_TURNED)
                    for q in range(QUADRANTS):
                        dst, src = kt_square(q, q)
                        act.activation(dst, src, ACT.Copy).then_inc(kt_diag, 1)
                take_u(3)
                take_u(DC)
                if prev:
                    act.wait_ge(kt_diag, QUADRANTS * s)
                    act.wait_ge(kt_off, QUADRANTS * s)
                    act.activation(KT_hi[:, :, :], KT[:, :, :], ACT.Copy).then_inc(kt_hi_ready, 1)
                if is_last(s - 1):
                    take_last_y(s - 1, TPB - 1)
                if live(s, -1):
                    split_hT(s + 1, 1 - p)
                take_u(DC + 1)
                take_u(DC + 2)
                take_u(DC + 3)
                out_tile(0)
                out_tile(1)
                out_tile(2)
                out_tile(3)
                if isinstance(s, int) and s == 0:
                    for i in range(DC):
                        act.wait_ge(proj_filled, 4 * DC + i + 1)
                        act.activation(MT_hi[:, i, :], ring[i % RING][:, :], ACT.Copy).then_inc(act_setup, 1)
                def scale_squares():
                    act.wait_ge(attn_step, ATTN_STEPS * s + SCALE_TURNED)
                    for q in range(QUADRANTS):
                        dst, src = scale_square(q, q)
                        act.activation(dst, src, ACT.Copy).then_inc(scale_own, 1)

                def exponentials():
                    act.wait_ge(attn_step, ATTN_STEPS * s + DIST)
                    act.activation(S[:, 1, :, :], S[:, 1, :, :], ACT.Exp, scale=neg_c[:, 0:1])\
                        .then_inc(exp_ready, 1)

                if is_last(s):
                    h1_tile(0)
                    h1_tile(1)
                    h1_tile(2)
                    h1_tile(3)
                    take_y(0)
                    scale_squares()
                    exponentials()
                    act.wait_ge(out_stored, 16 * (s - 1))
                    for t in range(1, TPB):
                        act.wait_ge(mix_filled, TPB * (s - 1) + t + 1)
                        act.activation(o[:, t, :], mix_bank[t], ACT.Copy).then_inc(mix_copied, 1)
                        if t < TPB - 1:
                            take_last_y(s, t)
                elif is_last(s - 1):
                    for half in range(2):
                        a, b = half * HALF, half * HALF + 1
                        act.wait_ge(ln_step[0], 4 * (s - 1) + 4 * (half + 1))
                        h1_hi_tile(a)
                        h1_hi_tile(b)
                        norm_tile(0, b, r[:, b, :], r[:, b, :], h1_ready)
                elif cur:
                    h1_tile(0)
                    h1_tile(1)
                    take_y(0)
                    h1_tile(2)
                    h1_tile(3)
                    take_y(1)
                    scale_squares()
                    exponentials()
                    take_y(2)
                    take_y(3)

            act.wait_ge(dve_setup, 9)
            pipeline(act, iteration)

        @block.vector
        def _(dve):
            def split_weight(n):
                for c in range(DC):
                    dve.wait_ge(w_hi_ready, n * DC + c + 1)
                    dve.tensor_tensor(w_lo[n][:, c, :], w_raw[n][:, c, :], w_hi[n][:, c, :].bitcast(fp32),
                                      ALU.subtract).then_inc(w_lo_ready, 1)

            split_weight(0)
            split_weight(1)
            split_weight(2)
            def small_constants():
                dve.wait_ge(small_loaded, 16 * SMALL_LOADS)
                dve.wait_ge(pool_setup, 3)
                dve.tensor_tensor(mask[:, :], adj2[:, :], eye[:, :], ALU.mult).then_inc(dve_setup, 1)
                dve.wait_ge(dve_setup, 1)
                dve.tensor_tensor(mask[:, :], adj2[:, :], mask[:, :], ALU.subtract).then_inc(dve_setup, 1)
                dve.tensor_tensor(adj2[:, :], adj2[:, :], adj2[:, :], ALU.mult).then_inc(dve_setup, 1)
                dve.wait_ge(dve_setup, 3)
                dve.tensor_scalar(ones[:, :], w_stage[0:1, 0, 0:PART], 0.0, 1.0, ALU.mult, ALU.add)
                dve.tensor_copy(bias_hi[:, :], bias_b[0:1, :]).then_inc(dve_setup, 1)
                for g in range(2):
                    rows = slice(g * NODES, (g + 1) * NODES)
                    dve.tensor_tensor(W1[rows, rows], adj2[rows, :], eye[rows, :],
                                      ALU.add).then_inc(dve_setup, 1)
                dve.wait_ge(dve_setup, 6)
                dve.tensor_tensor(bias_lo[:, :], bias_b[0:1, :], bias_hi[:, :].bitcast(fp32), ALU.subtract)
                dve.tensor_copy(W1_hi[:, :], W1[:, :]).then_inc(dve_setup, 1)
                dve.wait_ge(dve_setup, 7)
                dve.tensor_tensor(W1_lo[:, :], W1[:, :], W1_hi[:, :].bitcast(fp32), ALU.subtract)\
                    .then_inc(dve_setup, 1)
                dve.wait_ge(exps_ready, 2)
                dve.tensor_scalar(neg_c[:, :], wtmp[:, 1:2], -0.5, None, ALU.mult).then_inc(dve_setup, 1)
                dve.tensor_scalar(wtmp[:, 2:3], wtmp[:, 0:1], 1.0, None, ALU.add).then_inc(dve_setup, 1)
                dve.wait_ge(dve_setup, 10)
                dve.reciprocal(wtmp[:, 3:4], wtmp[:, 2:3]).then_inc(dve_setup, 1)
                dve.wait_ge(dve_setup, 11)
                dve.tensor_copy(gain[:, 0, :], wtmp[:, 3:4].to_broadcast([PART, TPB])).then_inc(dve_setup, 1)
                dve.wait_ge(dve_setup, 12)
                dve.tensor_scalar(gain[:, 1, :], gain[:, 0, :], -1.0, 1.0, ALU.mult, ALU.add)\
                    .then_inc(dve_setup, 1)

            fill, taken = 0, 0
            for w in range(2):
                if w == 1:
                    split_weight(3)
                for i in range(DC):
                    taken += 1 + (i < DC - 1)
                    dve.wait_ge(act_setup, taken)
                    diag = slice(tri(i, i), tri(i, i) + PART)
                    last = dve.scalar_tensor_tensor(U_lo[w][:, diag], ring[fill % RING][:, 0:PART], 0.5,
                                                    U_hi[w][:, diag].bitcast(fp32), ALU.mult, ALU.subtract)
                    if i < DC - 1:
                        rest = slice(tri(i, i) + PART, tri(i, i) + (DC - i) * PART)
                        last = dve.tensor_tensor(U_lo[w][:, rest], ring[fill % RING][:, PART:DIM - i * PART],
                                                 U_hi[w][:, rest].bitcast(fp32), ALU.subtract)
                    last.then_inc(proj_lo, 1)
                    fill += 1
            small_constants()
            setup_taken = taken

            def take_lo(s, n, dst, hi):
                dve.wait_ge(proj_hi, FILLS * s + n + 1)
                dve.tensor_tensor(dst, ring[n % RING][:, :], hi.bitcast(fp32), ALU.subtract)\
                    .then_inc(proj_lo, 1)

            eye_b = eye[:, :].unsqueeze(1).to_broadcast([PART, 2 * TPB, NODES])
            mask_t = mask[:, :].unsqueeze(1).to_broadcast([PART, TPB, NODES])

            def over_cols(v):
                return v.unsqueeze(2).to_broadcast([PART, v.shape[1], NODES])

            S_all = S[:, :, :, :].rearrange("p w t n -> p (w t) n")
            D_all = D[:, :, :, :].rearrange("p w t n -> p (w t) n")
            scale_all = scale[:, :, :].rearrange("p w t -> p (w t)")
            deg_all = deg[:, :, :].rearrange("p w t -> p (w t)")
            gain_all = gain[:, :, :].rearrange("p w t -> p (w t)")

            def iteration(s, p):
                cur, prev, prev2 = live(s, 0), live(s, 1), live(s, 2)

                def attn(k, step):
                    dve.wait_ge(attn_step, ATTN_STEPS * k + step)

                def take_u(n):
                    if cur:
                        take_lo(s, n, UT_lo[:, n % DC, n // DC, :], UT_hi[:, n % DC, n // DC, :])

                def take_y(t):
                    if cur:
                        take_lo(s, 2 * DC + t, y_lo[:, t, :], y_hi[:, t, :])

                def statistics(n, t, src):
                    dve.bn_stats(st[n][:, t, :], src).then_inc(stat[n], 1)

                def aggregate(n, tiles=range(TPB)):
                    for t in tiles:
                        dve.bn_aggr(mv[n][:, t, :], st[n][:, t, :]).then_inc(stat[n], 1)

                def residual(t):
                    if prev:
                        if t == 0:
                            dve.wait_ge(h_loaded, 16 * s)
                        dve.wait_ge(ky_filled, TPB * (s - 1) + t + 1)
                        dve.tensor_tensor(r[:, t, :], high2[:, t % 2, :], h[:, t, :], ALU.add)\
                            .then_inc(ky_taken, 1)

                def residual_statistics(t):
                    if prev:
                        dve.wait_ge(ky_taken, TPB * (s - 1) + t + 1)
                        statistics(0, t, r[:, t, :])

                def add_bias(t):
                    if prev:
                        if t == 0:
                            ge(dve, out_stored, 16 * (s - 1))
                        dve.wait_ge(mix_filled, TPB * (s - 1) + t + 1)
                        dve.tensor_tensor(o[:, t, :], mix_bank[t], bias_b[:, :], ALU.add)\
                            .then_inc(mix_taken, 1)

                def out_statistics(t):
                    if prev:
                        dve.wait_ge(mix_taken, TPB * (s - 1) + t + 1)
                        statistics(1, t, o[:, t, :])

                def attention_weights(k):
                    attn(k, COS)
                    dve.scalar_tensor_tensor(S[:, 0, :, :], S[:, 0, :, :], 0.0, mask_t, ALU.max, ALU.mult)\
                        .then_inc(attn_step, 1)
                    dve.wait_ge(exp_ready, k + 1)
                    dve.scalar_tensor_tensor(S[:, 1, :, :], S[:, 1, :, :], 1.0, mask_t, ALU.min, ALU.mult)\
                        .then_inc(attn_step, 1)
                    attn(k, A_GRAV)
                    dve.reduce_sum(deg_all, S_all, AX.X).then_inc(attn_step, 1)
                    attn(k, DEG)
                    dve.tensor_scalar(deg_all, deg_all, EPS, None, ALU.max).then_inc(attn_step, 1)
                    attn(k, DEG_MAX)
                    dve.reciprocal(deg_all, deg_all).then_inc(attn_step, 1)
                    attn(k, DEG_INV)
                    dve.tensor_tensor(deg_all, deg_all, gain_all, ALU.mult).then_inc(attn_step, 1)
                    attn(k, FACTOR)
                    dve.tensor_tensor(S_all, S_all, over_cols(deg_all), ALU.mult).then_inc(attn_step, 1)

                def turn_weights(k):
                    attn(k, SCALED)
                    dve.tensor_tensor(K[:, :, :], S[:, 0, :, :], S[:, 1, :, :], ALU.add).then_inc(attn_step, 1)
                    attn(k, K_SUM)
                    dve.transpose(K_turned[:, :, :], K[:, :, :]).then_inc(attn_step, 1)
                    attn(k, K_TURNED)
                    for q in range(QUADRANTS):
                        dst, src = kt_square(q, q ^ 1)
                        dve.tensor_copy(dst, src).then_inc(kt_off, 1)

                def halves(n, base, row_statistics):
                    for half in range(2):
                        tiles = range(half * HALF, (half + 1) * HALF)
                        for t in tiles:
                            row_statistics(t)
                        dve.wait_ge(stat[n], base + 2 * HALF * half + HALF)
                        dve.memset(anchor[:, :], 0.0)
                        aggregate(n, tiles)

                def last_h1():
                    def full(t):
                        dve.wait_ge(ln_step[0], 4 * (s - 1) + 4 * (t // HALF + 1))
                        dve.tensor_scalar(h1_full[:, t, :], r[:, t, :], rstd[0][:, t:t + 1],
                                          shift[0][:, t:t + 1], ALU.mult, ALU.add).then_inc(h1_full_dve, 1)

                    def rest(t, src, full_ready, full_count, hi_count):
                        dve.wait_ge(full_ready, full_count)
                        dve.wait_ge(h1_ready, hi_count)
                        dve.tensor_tensor(h1_lo[:, t, :], src[:, t, :], h1_hi[:, t, :].bitcast(fp32),
                                          ALU.subtract).then_inc(h1_lo_dve, 1)

                    full(0)
                    rest(0, h1_full, h1_full_dve, 1, LAST_H1 + 1)
                    rest(1, r, h1_ready, LAST_H1 + 3, LAST_H1 + 3)
                    full(2)
                    rest(2, h1_full, h1_full_dve, 2, LAST_H1 + 4)
                    rest(3, r, h1_ready, LAST_H1 + 6, LAST_H1 + 6)

                if prev2 and is_last(s - 2):
                    t = TPB - 1
                    dve.wait_ge(ln_step[1], 4 * (s - 2) + 8)
                    dve.tensor_scalar(o_last[:, t, :], mix_bank[t], rstd[1][:, t:t + 1], shift[1][:, t:t + 1],
                                      ALU.mult, ALU.add).then_inc(out_ready_dve, 1)

                def rest_of_out_statistics():
                    for t in range(1, TPB):
                        if is_last(s - 1):
                            dve.wait_ge(mix_biased, t)
                        else:
                            dve.wait_ge(mix_taken, TPB * (s - 2) + t + 1)
                        statistics(1, t, o[:, t, :])
                    dve.wait_ge(stat[1], 2 * TPB * (s - 2) + TPB)
                    dve.memset(anchor[:, :], 0.0)
                    aggregate(1)

                take_u(0)
                take_u(1)
                if prev and not is_last(s - 1):
                    turn_weights(s - 1)
                take_u(2)
                take_u(3)
                take_u(DC)
                if prev:
                    dve.wait_ge(kt_hi_ready, s)
                    dve.tensor_tensor(KT_lo[:, :, :], KT[:, :, :], KT_hi[:, :, :].bitcast(fp32), ALU.subtract)\
                        .then_inc(kt_lo_ready, 1)
                if prev2 and cur:
                    rest_of_out_statistics()
                take_u(DC + 1)
                take_u(DC + 2)
                if is_last(s - 1):
                    rest_of_out_statistics()
                take_u(DC + 3)
                if isinstance(s, int) and s == 0:
                    for i in range(DC):
                        dve.wait_ge(act_setup, setup_taken + i + 1)
                        dve.tensor_tensor(MT_lo[:, i, :], ring[i % RING][:, :],
                                          MT_hi[:, i, :].bitcast(fp32), ALU.subtract).then_inc(proj_lo, 1)
                if prev and is_last(s - 1):
                    def residual_and_statistics(t):
                        residual(t)
                        residual_statistics(t)

                    halves(0, 2 * TPB * (s - 1), residual_and_statistics)
                    last_h1()
                elif prev:
                    residual(0)
                    residual(1)
                    residual_statistics(0)
                    residual_statistics(1)
                    residual(2)
                    residual_statistics(2)
                    residual(3)
                    residual_statistics(3)
                    dve.wait_ge(stat[0], 2 * TPB * (s - 1) + TPB)
                    dve.memset(anchor[:, :], 0.0)
                    aggregate(0)

                def gram():
                    dve.wait_ge(gram_filled, s + 1)
                    for g in range(2):
                        rows = slice(g * NODES, (g + 1) * NODES)
                        dve.transpose(turned[rows, :, :, :], lowp[rows, :, :, rows]).then_inc(attn_step, 1)
                    attn(s, TURN_B)
                    for q in range(QUADRANTS):
                        g, rows = q // 2, slice(q * SQUARE, (q + 1) * SQUARE)
                        for c in range(2):
                            mirror = slice((2 * g + c) * SQUARE, (2 * g + c + 1) * SQUARE)
                            cols, turned_cols = slice(c * SQUARE, (c + 1) * SQUARE), slice(
                                q % 2 * SQUARE, (q % 2 + 1) * SQUARE)
                            dve.tensor_tensor(S[rows, :, :, cols].rearrange("p w t n -> p t w n"),
                                              lowp[rows, :, :, mirror], turned[mirror, :, :, turned_cols],
                                              ALU.add).then_inc(attn_step, 1)
                    attn(s, SUM)
                    dve.tensor_tensor(D_all, S_all, eye_b, ALU.mult).then_inc(attn_step, 1)
                    attn(s, DIAG)
                    dve.reduce_sum(scale_all, D_all, AX.X).then_inc(attn_step, 1)
                    attn(s, SQ)
                    dve.tensor_scalar(sq_max[:, :], scale[:, 0, :], EPS * EPS, None, ALU.max)\
                        .then_inc(attn_step, 1)
                    dve.scalar_tensor_tensor(S[:, 1, :, :], S[:, 1, :, :], -2.0, over_cols(scale[:, 1, :]),
                                             ALU.mult, ALU.add).then_inc(attn_step, 1)

                def scale_rows():
                    dve.wait_ge(rnorm_ready, s + 1)
                    dve.transpose(scale_turned[:, :, :, :].rearrange("p w t n -> p (w t) n"),
                                  scale_all.unsqueeze(2).to_broadcast([PART, 2 * TPB, SQUARE]))\
                        .then_inc(attn_step, 1)
                    dve.tensor_tensor(S[:, 0, :, :], S[:, 0, :, :], over_cols(scale[:, 0, :]), ALU.mult)\
                        .then_inc(attn_step, 1)

                def scale_columns():
                    attn(s, SCALE_TURNED)
                    for q in range(QUADRANTS):
                        dst, src = scale_square(q, q ^ 1)
                        dve.tensor_copy(dst, src).then_inc(scale_off, 1)
                    dve.wait_ge(scale_off, QUADRANTS * (s + 1))
                    dve.wait_ge(scale_own, QUADRANTS * (s + 1))
                    attn(s, COS_ROWS)
                    dve.tensor_tensor(S[:, 1, :, :], scale_cols[:, 1, :, :], S[:, 1, :, :], ALU.add)\
                        .then_inc(attn_step, 1)
                    dve.tensor_tensor(S[:, 0, :, :], scale_cols[:, 0, :, :], S[:, 0, :, :], ALU.mult)\
                        .then_inc(attn_step, 1)

                if is_last(s):
                    gram()
                    add_bias(0)
                    scale_rows()
                    take_y(0)
                    scale_columns()
                    attention_weights(s)
                    turn_weights(s)
                    out_statistics(0)
                elif is_last(s - 1):
                    def mix_statistics(t):
                        dve.wait_ge(mix_filled, TPB * (s - 1) + t + 1)
                        statistics(1, t, mix_bank[t])

                    halves(1, 2 * TPB * (s - 1), mix_statistics)
                elif cur:
                    gram()
                    take_y(0)
                    scale_rows()
                    scale_columns()
                    take_y(1)
                    add_bias(0)
                    add_bias(1)
                    take_y(2)
                    attention_weights(s)
                    take_y(3)
                    add_bias(2)
                    add_bias(3)
                    out_statistics(0)

            pipeline(dve, iteration)

        @block.gpsimd
        def _(pool):
            pool.memset(W1[:, :], 0.0).then_inc(pool_setup, 1)
            pool.memset(KT[:, :, :], 0.0).then_inc(pool_setup, 1)
            pool.memset(minus_half[:, :], -0.5).then_inc(pool_setup, 1)
            pool.memset(minus_one[:, :], -1.0).then_inc(pool_setup, 1)
            pool.memset(ln_eps[:, :], LN_EPS).then_inc(pool_setup, 1)
            pool.wait_ge(pool_setup, 5)

            def split_hT(k, p):
                pool.wait_ge(hT_hi_ready, k + 1)
                pool.tensor_tensor(hT_lo[p][:, :, :], hT[:, :, :], hT_hi[p][:, :, :].bitcast(fp32),
                                   ALU.subtract).then_inc(hT_lo_ready, 1)

            def norm_factors(n, k, tiles=range(TPB), part=0):
                sl = slice(tiles[0], tiles[-1] + 1)
                step = 4 * k + 4 * part
                pool.wait_ge(stat[n], 2 * TPB * k + 2 * len(tiles) * (part + 1))
                pool.tensor_tensor(var_e[n][:, sl], mv[n][:, sl, 1], ln_eps[:, sl], ALU.add)\
                    .then_inc(ln_step[n], 1)
                pool.tensor_tensor(neg_m[n][:, sl], mv[n][:, sl, 0], minus_one[:, sl], ALU.mult)\
                    .then_inc(ln_step[n], 1)
                pool.wait_ge(ln_step[n], step + 2)
                pool.tensor_tensor(rstd[n][:, sl], var_e[n][:, sl], minus_half[:, sl], ALU.pow)\
                    .then_inc(ln_step[n], 1)
                pool.wait_ge(ln_step[n], step + 3)
                pool.tensor_tensor(shift[n][:, sl], neg_m[n][:, sl], rstd[n][:, sl], ALU.mult)\
                    .then_inc(ln_step[n], 1)

            def norm_halves(n, k):
                for half in range(2):
                    norm_factors(n, k, range(half * HALF, (half + 1) * HALF), half)

            def iteration(s, p):
                cur, prev, prev2 = live(s, 0), live(s, 1), live(s, 2)

                def h1_rest(t):
                    if prev and not is_last(s - 1):
                        pool.wait_ge(h1_ready, 2 * (TPB * (s - 1) + t + 1))
                        pool.tensor_tensor(h1_lo[:, t, :], r[:, t, :], h1_hi[:, t, :].bitcast(fp32),
                                           ALU.subtract).then_inc(h1_lo_ready, 1)

                if prev2 and is_last(s - 2):
                    norm_halves(1, s - 2)
                elif prev2:
                    norm_factors(1, s - 2)
                if live(s, -1):
                    split_hT(s + 1, 1 - p)
                if prev and is_last(s - 1):
                    norm_halves(0, s - 1)
                elif prev:
                    norm_factors(0, s - 1)
                def inverse_norms():
                    pool.wait_ge(attn_step, ATTN_STEPS * s + SQ_MAX)
                    pool.tensor_tensor(scale[:, 0, :], sq_max[:, :], minus_half[:, :], ALU.pow)\
                        .then_inc(rnorm_ready, 1)

                h1_rest(0)
                h1_rest(1)
                if cur:
                    inverse_norms()
                h1_rest(2)
                h1_rest(3)
                if is_last(s):
                    for t in range(1, TPB):
                        pool.wait_ge(mix_copied, t)
                        pool.tensor_tensor(o[:, t, :], o[:, t, :], bias_b[:, :], ALU.add)\
                            .then_inc(mix_biased, 1)
                        pool.wait_ge(y_copied, t)
                        pool.tensor_tensor(y_lo[:, t, :], y_last[:, t, :], y_hi[:, t, :].bitcast(fp32),
                                           ALU.subtract).then_inc(y_lo_pool, 1)

            split_hT(0, 0)
            pipeline(pool, iteration)


def kernel(x, adj, L0_gnn_W_lang, L0_gnn_W_grav, L0_gnn_W_V, L0_gnn_W_O, L0_gnn_gate_logit,
           L0_gnn_log_sigma, L1_gnn_bias):
    import numpy as np
    import concourse.bacc as bacc
    from concourse.bass_utils import run_bass_kernel_spmd

    x = np.ascontiguousarray(x).reshape(TOKENS, DIM)
    arrays = {
        "x": x,
        "xT": np.ascontiguousarray(x.reshape(NB, BLOCK, DC, PART).transpose(0, 3, 2, 1)),
        "adj": np.ascontiguousarray(adj),
        "w_lang": np.ascontiguousarray(L0_gnn_W_lang),
        "w_grav": np.ascontiguousarray(L0_gnn_W_grav),
        "w_v": np.ascontiguousarray(L0_gnn_W_V),
        "w_oT": np.ascontiguousarray(np.asarray(L0_gnn_W_O).T),
        "gate": np.asarray(L0_gnn_gate_logit).reshape(1, 1),
        "log_sigma": np.asarray(L0_gnn_log_sigma).reshape(1, 1),
        "bias": np.ascontiguousarray(L1_gnn_bias).reshape(1, DIM),
        "eyes": np.concatenate([np.eye(NODES, dtype=np.float32)] * (PART // NODES)),
    }
    nc = bacc.Bacc("TRN2", target_bir_lowering=False, num_devices=1)
    aps = {n: nc.dram_tensor(n, a.shape, mybir.dt.from_np(a.dtype), kind="ExternalInput").ap()
           for n, a in arrays.items()}
    aps["out"] = nc.dram_tensor("out", (TOKENS, DIM), mybir.dt.float32, kind="ExternalOutput").ap()
    build(nc, **aps)
    res = run_bass_kernel_spmd(nc, [arrays], core_ids=[0])
    return res.results[0]["out"].reshape(GRAPHS, NODES, DIM)
```
